# Optimizing a Trainium2 kernel written in Bass

```python
import numpy as np
import jax
import jax.numpy as jnp

def _softmax(x, axis=-1):
    return jax.nn.softmax(x, axis=axis)

def _gelu(x):
    return jax.nn.gelu(x, approximate=True)

def _silu(x):
    return jax.nn.silu(x)

def _sigmoid(x):
    return jax.nn.sigmoid(x)

def _layernorm(x, axis=-1, eps=1e-05):
    m = jnp.mean(x, axis=axis, keepdims=True)
    v = jnp.var(x, axis=axis, keepdims=True)
    return (x - m) / jnp.sqrt(v + eps)

def _scatter_add(tgt, idx, src, axis=0):
    return tgt.at[idx].add(src)

def _segment_sum(src, seg, n):
    return jax.ops.segment_sum(src, seg, n)
kernel_name = 'mk_vit_tower_postln_d1_tok_img512_r4_fbab72'

def setup_inputs(seed: int=0):
    np.random.seed(seed)
    _w = jnp.asarray

    def _rec_inputs():
        import jax
        import jax.numpy as jnp
        _rk = jax.random.key(seed)
        x = 7.57192e-06 + 1.00007 * jax.random.normal(jax.random.fold_in(_rk, 1), (64, 84, 84, 3), jnp.float32)
        return x
    x = _rec_inputs()

    def _L0_tok_setup():
        import jax, jax.numpy as jnp
        import numpy as np
        B, H, W, C = (64, 224, 224, 3)
        P, D = (16, 128)
        LN_EPS = 0.001

        def _shift4(x):
            pad = lambda a, spec: jnp.pad(a, spec)
            right = pad(x[:, :, :-1, :], ((0, 0), (0, 0), (1, 0), (0, 0)))
            left = pad(x[:, :, 1:, :], ((0, 0), (0, 0), (0, 1), (0, 0)))
            down = pad(x[:, :-1, :, :], ((0, 0), (1, 0), (0, 0), (0, 0)))
            up = pad(x[:, 1:, :, :], ((0, 0), (0, 1), (0, 0), (0, 0)))
            return [right, left, down, up]
        key = jax.random.key(seed)
        k0, k1, k2 = jax.random.split(key, 3)
        x = jax.random.normal(k0, (B, H, W, C), jnp.float32)
        conv_w = jax.random.normal(k1, (P, P, 5 * C, D), jnp.float32) * 0.02
        conv_b = jnp.zeros((D,), jnp.float32)
        gamma = jnp.ones((D,), jnp.float32)
        beta = jnp.zeros((D,), jnp.float32)
        dense_w = jax.random.normal(k2, (D, D), jnp.float32) * 0.02
        dense_b = jnp.zeros((D,), jnp.float32)
        return {'x': x, 'conv_w': conv_w, 'conv_b': conv_b, 'gamma': gamma, 'beta': beta, 'dense_w': dense_w, 'dense_b': dense_b}
    _L0_tok_all = _L0_tok_setup()
    _L0_tok_in = {k: v for k, v in _L0_tok_all.items() if k in ('conv_w', 'conv_b', 'gamma', 'beta', 'dense_w', 'dense_b')}
    del _L0_tok_all

    def _L0_attn_setup():
        import jax, jax.numpy as jnp
        import numpy as np
        B, S, D = (2, 512, 128)
        H = 8
        G = 4
        LAMBDA_INIT = 0.2
        EPS = 1e-05
        key = jax.random.key(seed)
        ks = jax.random.split(key, 16)
        n = jax.random.normal
        return {'x': n(ks[0], (B, S, D), jnp.float32), 'K1_w': n(ks[1], (D, D), jnp.float32) * 0.02, 'K1_b': n(ks[2], (D,), jnp.float32) * 0.02, 'Q1_w': n(ks[3], (D, D), jnp.float32) * 0.02, 'K2_w': n(ks[4], (D, D), jnp.float32) * 0.02, 'K2_b': n(ks[5], (D,), jnp.float32) * 0.02, 'Q2_w': n(ks[6], (D, D), jnp.float32) * 0.02, 'V_w': n(ks[7], (D, D), jnp.float32) * 0.02, 'lambda_q1': n(ks[8], (H, 1), jnp.float32), 'lambda_k1': n(ks[9], (H, 1), jnp.float32), 'lambda_q2': n(ks[10], (H, 1), jnp.float32), 'lambda_k2': n(ks[11], (H, 1), jnp.float32), 'gn_w': jnp.ones((D,), jnp.float32), 'gn_b': jnp.zeros((D,), jnp.float32), 'out_w': n(ks[12], (D, D), jnp.float32) * 0.02, 'out_b': n(ks[13], (D,), jnp.float32) * 0.02}
    _L0_attn_all = _L0_attn_setup()
    _L0_attn_in = {k: v for k, v in _L0_attn_all.items() if k in ('K1_w', 'K1_b', 'Q1_w', 'K2_w', 'K2_b', 'Q2_w', 'V_w', 'lambda_q1', 'lambda_k1', 'lambda_q2', 'lambda_k2', 'gn_w', 'gn_b', 'out_w', 'out_b')}
    del _L0_attn_all

    def _L0_ffn_setup():
        import jax, jax.numpy as jnp
        import numpy as np
        B, S, D, F, E = (8, 1024, 128, 512, 8)
        INIT_LAMBDA = 0.2
        LN_EPS = 1e-05
        LN_MERGE = 0.03
        key = jax.random.key(seed)
        ks = jax.random.split(key, 12)
        n = lambda k, shp, s=1.0: jax.random.normal(k, shp, dtype=jnp.float32) * s
        return {'hidden_states': n(ks[0], (B, S, D)), 'gfc1_w': n(ks[1], (D, D), 0.01), 'gfc1_b': jnp.zeros((D,), jnp.float32), 'gfc2_w': n(ks[2], (E, D), 0.01), 'gfc2_b': jnp.full((E,), INIT_LAMBDA, dtype=jnp.float32), 'W1': n(ks[3], (F, D), 0.02), 'b1': jnp.zeros((F,), jnp.float32), 'W2': n(ks[4], (D, F), 0.02), 'b2': jnp.zeros((D,), jnp.float32), 'ln_g': jnp.ones((D,), jnp.float32), 'ln_b': jnp.zeros((D,), jnp.float32), 'tv_W1': n(ks[5], (E, F, D), 0.02), 'tv_b1': n(ks[6], (E, F), 0.02), 'tv_W2': n(ks[7], (E, D, F), 0.02), 'tv_b2': n(ks[8], (E, D), 0.02), 'tv_ln_g': n(ks[9], (E, D), 0.02), 'tv_ln_b': n(ks[10], (E, D), 0.02)}
    _L0_ffn_all = _L0_ffn_setup()
    _L0_ffn_in = {k: v for k, v in _L0_ffn_all.items() if k in ('gfc1_w', 'gfc1_b', 'gfc2_w', 'gfc2_b', 'W1', 'b1', 'W2', 'b2', 'ln_g', 'ln_b', 'tv_W1', 'tv_b1', 'tv_W2', 'tv_b2', 'tv_ln_g', 'tv_ln_b')}
    del _L0_ffn_all
    return {'x': x, 'L0_tok_conv_w': _L0_tok_in['conv_w'], 'L0_tok_conv_b': _L0_tok_in['conv_b'], 'L0_tok_gamma': _L0_tok_in['gamma'], 'L0_tok_beta': _L0_tok_in['beta'], 'L0_tok_dense_w': _L0_tok_in['dense_w'], 'L0_tok_dense_b': _L0_tok_in['dense_b'], 'L0_attn_K1_w': _L0_attn_in['K1_w'], 'L0_attn_K1_b': _L0_attn_in['K1_b'], 'L0_attn_Q1_w': _L0_attn_in['Q1_w'], 'L0_attn_K2_w': _L0_attn_in['K2_w'], 'L0_attn_K2_b': _L0_attn_in['K2_b'], 'L0_attn_Q2_w': _L0_attn_in['Q2_w'], 'L0_attn_V_w': _L0_attn_in['V_w'], 'L0_attn_lambda_q1': _L0_attn_in['lambda_q1'], 'L0_attn_lambda_k1': _L0_attn_in['lambda_k1'], 'L0_attn_lambda_q2': _L0_attn_in['lambda_q2'], 'L0_attn_lambda_k2': _L0_attn_in['lambda_k2'], 'L0_attn_gn_w': _L0_attn_in['gn_w'], 'L0_attn_gn_b': _L0_attn_in['gn_b'], 'L0_attn_out_w': _L0_attn_in['out_w'], 'L0_attn_out_b': _L0_attn_in['out_b'], 'L0_ffn_gfc1_w': _L0_ffn_in['gfc1_w'], 'L0_ffn_gfc1_b': _L0_ffn_in['gfc1_b'], 'L0_ffn_gfc2_w': _L0_ffn_in['gfc2_w'], 'L0_ffn_gfc2_b': _L0_ffn_in['gfc2_b'], 'L0_ffn_W1': _L0_ffn_in['W1'], 'L0_ffn_b1': _L0_ffn_in['b1'], 'L0_ffn_W2': _L0_ffn_in['W2'], 'L0_ffn_b2': _L0_ffn_in['b2'], 'L0_ffn_ln_g': _L0_ffn_in['ln_g'], 'L0_ffn_ln_b': _L0_ffn_in['ln_b'], 'L0_ffn_tv_W1': _L0_ffn_in['tv_W1'], 'L0_ffn_tv_b1': _L0_ffn_in['tv_b1'], 'L0_ffn_tv_W2': _L0_ffn_in['tv_W2'], 'L0_ffn_tv_b2': _L0_ffn_in['tv_b2'], 'L0_ffn_tv_ln_g': _L0_ffn_in['tv_ln_g'], 'L0_ffn_tv_ln_b': _L0_ffn_in['tv_ln_b']}

def reference(x, L0_tok_conv_w, L0_tok_conv_b, L0_tok_gamma, L0_tok_beta, L0_tok_dense_w, L0_tok_dense_b, L0_attn_K1_w, L0_attn_K1_b, L0_attn_Q1_w, L0_attn_K2_w, L0_attn_K2_b, L0_attn_Q2_w, L0_attn_V_w, L0_attn_lambda_q1, L0_attn_lambda_k1, L0_attn_lambda_q2, L0_attn_lambda_k2, L0_attn_gn_w, L0_attn_gn_b, L0_attn_out_w, L0_attn_out_b, L0_ffn_gfc1_w, L0_ffn_gfc1_b, L0_ffn_gfc2_w, L0_ffn_gfc2_b, L0_ffn_W1, L0_ffn_b1, L0_ffn_W2, L0_ffn_b2, L0_ffn_ln_g, L0_ffn_ln_b, L0_ffn_tv_W1, L0_ffn_tv_b1, L0_ffn_tv_W2, L0_ffn_tv_b2, L0_ffn_tv_ln_g, L0_ffn_tv_ln_b):
    import jax
    import jax.numpy as jnp

    def _L0_tok_ref(x, conv_w, conv_b, gamma, beta, dense_w, dense_b):
        import jax, jax.numpy as jnp
        import numpy as np
        B, H, W, C = (64, 224, 224, 3)
        P, D = (16, 128)
        LN_EPS = 0.001

        def _shift4(x):
            pad = lambda a, spec: jnp.pad(a, spec)
            right = pad(x[:, :, :-1, :], ((0, 0), (0, 0), (1, 0), (0, 0)))
            left = pad(x[:, :, 1:, :], ((0, 0), (0, 0), (0, 1), (0, 0)))
            down = pad(x[:, :-1, :, :], ((0, 0), (1, 0), (0, 0), (0, 0)))
            up = pad(x[:, 1:, :, :], ((0, 0), (0, 1), (0, 0), (0, 0)))
            return [right, left, down, up]
        xs = jnp.concatenate([x, *_shift4(x)], axis=-1)
        y = jax.lax.conv_general_dilated(xs, conv_w, window_strides=(P, P), padding='VALID', dimension_numbers=('NHWC', 'HWIO', 'NHWC')) + conv_b
        y = y.reshape(y.shape[0], -1, D)
        mu = jnp.mean(y, axis=-1, keepdims=True)
        var = jnp.mean(jnp.square(y - mu), axis=-1, keepdims=True)
        y = (y - mu) * jax.lax.rsqrt(var + LN_EPS) * gamma + beta
        return y @ dense_w + dense_b

    def _L0_attn_ref(x, K1_w, K1_b, Q1_w, K2_w, K2_b, Q2_w, V_w, lambda_q1, lambda_k1, lambda_q2, lambda_k2, gn_w, gn_b, out_w, out_b):
        import jax, jax.numpy as jnp
        import numpy as np
        B, S, D = (2, 512, 128)
        H = 8
        G = 4
        LAMBDA_INIT = 0.2
        EPS = 1e-05
        b, s, d = x.shape
        hd = d // H

        def heads(t):
            return t.reshape(b, s, H, hd).transpose(0, 2, 1, 3)
        q1 = heads(x @ Q1_w.T)
        k1 = heads(x @ K1_w.T + K1_b)
        q2 = heads(x @ Q2_w.T)
        k2 = heads(x @ K2_w.T + K2_b)
        v = heads(x @ V_w.T)
        scale = hd ** 0.5
        a1 = jax.nn.softmax(jnp.einsum('bhqd,bhkd->bhqk', q1, k1) / scale, axis=-1)
        a2 = jax.nn.softmax(jnp.einsum('bhqd,bhkd->bhqk', q2, k2) / scale, axis=-1)
        lam = jnp.exp(lambda_q1 * lambda_k1) - jnp.exp(lambda_q2 * lambda_k2) + LAMBDA_INIT
        attn = a1 - lam.reshape(1, H, 1, 1) * a2
        o = jnp.einsum('bhqk,bhkd->bhqd', attn, v)
        o = o.transpose(0, 2, 1, 3).reshape(b, s, d)
        xc = o.transpose(0, 2, 1).reshape(b, G, d // G, s)
        mu = xc.mean(axis=(2, 3), keepdims=True)
        var = xc.var(axis=(2, 3), keepdims=True)
        xn = ((xc - mu) * jax.lax.rsqrt(var + EPS)).reshape(b, d, s)
        xn = xn * gn_w[None, :, None] + gn_b[None, :, None]
        y = xn.transpose(0, 2, 1) @ out_w.T + out_b
        return y

    def _L0_ffn_ref(hidden_states, gfc1_w, gfc1_b, gfc2_w, gfc2_b, W1, b1, W2, b2, ln_g, ln_b, tv_W1, tv_b1, tv_W2, tv_b2, tv_ln_g, tv_ln_b):
        import jax, jax.numpy as jnp
        import numpy as np
        B, S, D, F, E = (8, 1024, 128, 512, 8)
        INIT_LAMBDA = 0.2
        LN_EPS = 1e-05
        LN_MERGE = 0.03
        x = hidden_states
        gh = jax.nn.relu(jnp.einsum('bsd,hd->bsh', x, gfc1_w) + gfc1_b)
        g = (jnp.einsum('bsh,eh->bse', gh, gfc2_w) + gfc2_b).mean(axis=1)
        W1m = W1 + jnp.einsum('be,efd->bfd', g, tv_W1)
        b1m = b1 + g @ tv_b1
        W2m = W2 + jnp.einsum('be,edf->bdf', g, tv_W2)
        b2m = b2 + g @ tv_b2
        lng = ln_g + LN_MERGE * (tv_ln_g - ln_g).sum(axis=0)
        lnb = ln_b + LN_MERGE * (tv_ln_b - ln_b).sum(axis=0)
        h = jax.nn.relu(jnp.einsum('bsd,bfd->bsf', x, W1m) + b1m[:, None, :])
        out = jnp.einsum('bsf,bdf->bsd', h, W2m) + b2m[:, None, :]
        res = x + out
        mu = res.mean(axis=-1, keepdims=True)
        var = res.var(axis=-1, keepdims=True)
        return (res - mu) * jax.lax.rsqrt(var + LN_EPS) * lng + lnb
    h = _L0_tok_ref(x, L0_tok_conv_w, L0_tok_conv_b, L0_tok_gamma, L0_tok_beta, L0_tok_dense_w, L0_tok_dense_b)
    h = _layernorm(h + _L0_attn_ref(h, L0_attn_K1_w, L0_attn_K1_b, L0_attn_Q1_w, L0_attn_K2_w, L0_attn_K2_b, L0_attn_Q2_w, L0_attn_V_w, L0_attn_lambda_q1, L0_attn_lambda_k1, L0_attn_lambda_q2, L0_attn_lambda_k2, L0_attn_gn_w, L0_attn_gn_b, L0_attn_out_w, L0_attn_out_b), axis=-1)
    h = _layernorm(h + _L0_ffn_ref(h, L0_ffn_gfc1_w, L0_ffn_gfc1_b, L0_ffn_gfc2_w, L0_ffn_gfc2_b, L0_ffn_W1, L0_ffn_b1, L0_ffn_W2, L0_ffn_b2, L0_ffn_ln_g, L0_ffn_ln_b, L0_ffn_tv_W1, L0_ffn_tv_b1, L0_ffn_tv_W2, L0_ffn_tv_b2, L0_ffn_tv_ln_g, L0_ffn_tv_ln_b), axis=-1)
    return h

_drawn_inputs = setup_inputs


def setup_inputs(seed=0):
    import zlib

    import numpy as np

    out = dict(_drawn_inputs(seed))
    spreads = {'L0_tok_conv_b': (0.0, 0.1),
     'L0_tok_gamma': (1.0, 0.2),
     'L0_tok_beta': (0.0, 0.1),
     'L0_tok_dense_b': (0.0, 0.1),
     'L0_attn_gn_w': (1.0, 0.2),
     'L0_attn_gn_b': (0.0, 0.1),
     'L0_ffn_gfc1_b': (0.0, 0.8),
     'L0_ffn_gfc2_b': (0.20000000298023224, 0.6),
     'L0_ffn_b1': (0.0, 0.532),
     'L0_ffn_b2': (0.0, 0.278),
     'L0_ffn_ln_g': (1.0, 0.2),
     'L0_ffn_ln_b': (0.0, 0.1)}
    factors = {'L0_attn_K1_w': 8.0,
     'L0_attn_K1_b': 64.0,
     'L0_attn_Q1_w': 8.0,
     'L0_attn_K2_w': 8.0,
     'L0_attn_K2_b': 64.0,
     'L0_attn_Q2_w': 8.0,
     'L0_ffn_gfc1_w': 8.0,
     'L0_ffn_gfc2_w': 8.0,
     'L0_ffn_tv_W1': 3.266,
     'L0_ffn_tv_b1': 8.0,
     'L0_ffn_tv_W2': 2.738,
     'L0_ffn_tv_b2': 8.0,
     'L0_ffn_tv_ln_g': 53.188,
     'L0_ffn_tv_ln_b': 58.314}
    for name, (base, spread) in spreads.items():
        noise = np.random.default_rng([zlib.crc32(name.encode()), seed]).standard_normal(out[name].shape)
        drawn = base * np.exp(spread * noise) if base else spread * noise
        out[name] = jnp.asarray(drawn.astype(out[name].dtype))
    for name, factor in factors.items():
        out[name] = (out[name] * factor).astype(out[name].dtype)
    return out
```

```python
import concourse.bass as bass
from concourse import mybir
from contextlib import ExitStack

P = 128
NI, NS = 64, 25
NTOK = NI * NS
D, H, HD = 128, 8, 16
F, NE = 512, 8
KT = 8
NSH = 5
TM = 128
ST = 2 * TM
NSTEP = -(-NTOK // ST)
NTILE = -(-NTOK // TM)
NQ = 4
QI, QT = NI // NQ, NTOK // NQ
NG = NI // 4
NJ = 8
R = (NE + 1) * NJ
SJ = P // NJ
NC = F // P
HC = NS + 1
PAD = 8

_COLS = [("dense_w", 128), ("q1", 128), ("k1", 128), ("q2", 128), ("k2", 128), ("v", 128), ("o", 128),
         ("gfc1", 128), ("gfc2", R), ("gamma", 1), ("beta", 1), ("dense_b", 1), ("k1_b", 1), ("k2_b", 1),
         ("gn_w", 1), ("gn_b", 1), ("out_b", 1), ("gfc1_b", 1), ("gate_b", 1), ("even", 1), ("odd", 1),
         ("slice", NJ), ("tvb1", F), ("tvb2", D), ("ln_g", D), ("ln_b", D), ("coef", 128),
         ("gnsum", 128), ("ident", 128), ("lam", 4 * H)]
COL, _at = {}, 0
for _n, _w in _COLS:
    COL[_n] = (_at, _at + _w)
    _at += _w
NCONST = _at


def step_tokens(s):
    n = min(ST, NTOK - s * ST)
    return n, min(n, TM), -(-n // TM)


def build(nc, cst_d, wconv_d, xcol_d, tvw1_d, tvw2_d, out_d):
    f32 = mybir.dt.float32
    ALU = mybir.AluOpType
    ACT = mybir.ActivationFunctionType
    AX = mybir.AxisListType
    ctx = ExitStack()
    with ctx:
        def sb(name, cols, rows=P):
            return ctx.enter_context(nc.sbuf_tensor(name, [rows, cols], f32))

        def sem(name):
            return ctx.enter_context(nc.semaphore(name))

        cst = sb("cst", NCONST)
        arena = sb("arena", 2 * NI * P)
        hid = sb("hid", NC * NI * HC)
        tvw = [sb("tvw1", NC * SJ * P, R), sb("tvw2", NC * SJ * P, R)]
        t1 = sb("t1", NTILE * TM)
        t2 = sb("t2", NTILE * TM)
        t3 = sb("t3", NTILE * TM)
        t4 = sb("t4", NTILE * TM)
        t5 = sb("t5", NTILE * TM)
        t6 = sb("t6", NTILE * TM)
        PS = ctx.enter_context(nc.psum_tensor("PS", [P, 8, 512], f32))

        def C(name, rows=P):
            a, b = COL[name]
            return cst[0:rows, a:b]

        def xs(s):
            n = step_tokens(s)[0]
            return arena[:, KT * ST * s:KT * ST * s + KT * n].rearrange("p (k n) -> p k n", k=KT)

        w5 = hid[:, 0:KT * NSH * D]
        weff = hid[:, KT * NSH * D:KT * (NSH + 1) * D].rearrange("p (k d) -> p k d", k=KT)
        at = [0]

        def take(n):
            at[0] += n
            assert at[0] <= 2 * NI * P
            return arena[:, at[0] - n:at[0]]
        qT = [take(NTOK + PAD) for _ in range(2)]
        kX = [take(2 * NTOK).rearrange("p (b m k) -> p b m k", m=2, k=NS) for _ in range(2)]
        vtok = take(NG * D).rearrange("p (g c) -> p g c", g=NG)
        UC = 4 * 2 * 2 * NS
        E = take(4 * UC).rearrange("p (u c) -> p u c", u=4)
        prob = take(2 * 4 * H * 32).rearrange("p (n g h k) -> p n g h k", n=2, g=4, h=H)
        probT = hid[:, 0:2 * 4 * H * 32].rearrange("p (n g h q) -> p n g h q", n=2, g=4, h=H)
        otmp = hid[:, 2048:2048 + QT].rearrange("p (i g q) -> p i g q", i=4, g=4)
        gns = hid[:, 3000:3000 + 4 * NI].rearrange("p (a b) -> p a b", a=4)
        wm = [arena[:, i * NI * P:(i + 1) * NI * P].rearrange("p (b m) -> p b m", b=NI) for i in range(2)]
        hidv = hid[:, :].rearrange("p (c b k) -> p c b k", c=NC, k=HC)
        gates = t4[0:R, 0:NJ * NI].rearrange("p (j b) -> p j b", j=NJ)
        nb1 = t4[:, 512:512 + NC * NI].rearrange("p (c b) -> p c b", c=NC)
        gate1 = t4[0:R, 768:768 + NI]
        ghsum = t4[:, 832:832 + NI]

        mx = sb("mx", 64)
        sm = sb("sm", 64)
        rec = sb("rec", 64)
        wr = sb("wr", 64)
        lamw = sb("lamw", 64)
        lprod = sb("lprod", 2 * H)
        lexp = sb("lexp", 2 * H)
        neglam = sb("neglam", 2 * H)
        kb = sb("kb", 4)
        epsc = sb("epsc", 2)
        obias = sb("obias", 1)
        lnaff = sb("lnaff", 2 * D)
        st = [sb(f"st{i}", NTILE * 6) for i in range(4)]
        mv = [sb(f"mv{i}", NTILE * 2) for i in range(4)]
        sd = [sb(f"sd{i}", NTILE) for i in range(4)]
        rs = [sb(f"rs{i}", NTILE) for i in range(4)]

        w_loaded = [sem(f"w_loaded{i}") for i in range(2)]
        x_loaded = [sem(f"x_loaded{i}") for i in range(NSTEP)]
        cst_loaded = sem("cst_loaded")
        tv_loaded = [sem("tv1_loaded"), sem("tv2_loaded")]
        stored = sem("stored")
        weff_ready = sem("weff_ready")
        conv_done = sem("conv_done")
        eps_set = sem("eps_set")
        stats_done = [sem(f"stats_done{i}") for i in range(4)]
        aggr_done = [sem(f"aggr_done{i}") for i in range(4)]
        sd_done = [sem(f"sd_done{i}") for i in range(4)]
        rstd_done = [sem(f"rstd_done{i}") for i in range(4)]
        norm_done = [sem(f"norm_done{i}") for i in range(4)]
        trans_done = [sem(f"trans_done{i}") for i in range(3)]
        z_ready = sem("z_ready")
        dense_done = sem("dense_done")
        h_ready = sem("h_ready")
        small_done = sem("small_done")
        obias_ready = sem("obias_ready")
        lnaff_ready = sem("lnaff_ready")
        kb_ready = sem("kb_ready")
        pads_set = sem("pads_set")
        probs_zeroed = sem("probs_zeroed")
        proj_done = [sem(f"proj_done{w}") for w in range(4)]
        proj_ready = [sem(f"proj_ready{w}") for w in range(4)]
        v_done = sem("v_done")
        v_ready = [sem("v_ready_act"), sem("v_ready_dve")]
        lprod_ready = sem("lprod_ready")
        lexp_ready = sem("lexp_ready")
        neglam_ready = sem("neglam_ready")
        lamw_ready = sem("lamw_ready")
        hb_ready = sem("hb_ready")
        scores_done = sem("scores_done")
        max_done = sem("max_done")
        shifted = sem("shifted")
        exp_done = sem("exp_done")
        sum_done = sem("sum_done")
        rec_done = sem("rec_done")
        wr_done = sem("wr_done")
        scaled = sem("scaled")
        prob_done = sem("prob_done")
        probT_done = sem("probT_done")
        pv_done = sem("pv_done")
        otmp_done = sem("otmp_done")
        o_ready = sem("o_ready")
        gsum_done = sem("gsum_done")
        gmean_done = sem("gmean_done")
        gcent_done = sem("gcent_done")
        gsq_done = sem("gsq_done")
        gsqsum_done = sem("gsqsum_done")
        gvar_done = sem("gvar_done")
        gsd_done = sem("gsd_done")
        grstd_done = sem("grstd_done")
        xn_ready = sem("xn_ready")
        attn_done = sem("attn_done")
        x2_ready = sem("x2_ready")
        gfc1_done = sem("gfc1_done")
        gh_ready = sem("gh_ready")
        ghsum_done = sem("ghsum_done")
        gfc2_done = sem("gfc2_done")
        gate1_done = sem("gate1_done")
        gates_ready = sem("gates_ready")
        b1_done = sem("b1_done")
        b1_ready = sem("b1_ready")
        b1col_ready = sem("b1col_ready")
        merge_done = sem("merge_done")
        merged = [sem("merged_by_dve"), sem("merged_by_act")]
        applied = sem("applied")
        pre_done = sem("pre_done")
        hid_ready = sem("hid_ready")
        ffn_done = sem("ffn_done")
        res_part = sem("res_part")
        res_ready = sem("res_ready")
        x2b_ready = sem("x2b_ready")
        aff_part = sem("aff_part")
        aff_done = sem("aff_done")

        ident = C("ident")
        steps_for = [-(-min(NTOK, QT * (c + 1)) // ST) for c in range(NQ)]
        res_for = [-(-min(NTOK, ST * (s + 1)) // QT) for s in range(NSTEP)]
        bank2 = [4, 5, 6, 7, 0, 1, 2]

        def merged_views(m):
            cc, k = m // 8, m % 8
            b0 = 2 * (m % 2)
            src = PS[:, b0:b0 + 2, :].rearrange("p s (j b) -> p s j b", j=NJ)
            dst = wm[cc % 2].rearrange("p b (j s) -> p s j b", j=NJ)[:, 2 * k:2 * k + 2]
            return src, dst

        def weights_free(eng, cc):
            if cc - 2 < NC:
                eng.wait_ge(pre_done, NQ * (cc - 1))
            else:
                eng.wait_ge(applied, cc - 1 - NC)

        def evac_merged(eng, m):
            src, dst = merged_views(m)
            if m % 2:
                return eng.activation(dst, src, ACT.Copy)
            return eng.tensor_copy(dst, src)

        block = ctx.enter_context(nc.Block())

        @block.sync
        def _(sp):
            half = KT // 2 * NSH * D
            sp.dma_start(w5[:, 0:half], wconv_d[:, 0:half]).then_inc(w_loaded[0], 16)
            sp.dma_start(xs(0), xcol_d[0]).then_inc(x_loaded[0], 16)
            sp.dma_start(w5[:, half:2 * half], wconv_d[:, half:2 * half]).then_inc(w_loaded[1], 16)
            sp.dma_start(cst[:, :], cst_d).then_inc(cst_loaded, 16)
            for s in range(1, NSTEP):
                sp.dma_start(xs(s), xcol_d[s]).then_inc(x_loaded[s], 16)
            sp.dma_start(tvw[0][:, :], tvw1_d).then_inc(tv_loaded[0], 16)
            sp.dma_start(tvw[1][:, :], tvw2_d).then_inc(tv_loaded[1], 16)
            for s in range(NSTEP):
                n, rows, nt = step_tokens(s)
                sp.wait_ge(norm_done[3], min(2 * s + nt, NTILE))
                dst = out_d[s * ST:s * ST + n, :].rearrange("(t p) d -> p t d", p=rows)
                src = t5[0:rows, s * ST:s * ST + nt * TM].rearrange("p (t d) -> p t d", t=nt)
                sp.dma_start(dst, src).then_inc(stored, 16)
            sp.wait_ge(stored, 16 * NSTEP)

        @block.gpsimd
        def _(pool):
            pool.memset(epsc[:, 0:1], 1e-3).then_inc(eps_set, 1)
            pool.memset(epsc[:, 1:2], 1e-5).then_inc(eps_set, 1)
            pool.memset(t2[:, NTOK:NTOK + PAD], 0.0).then_inc(pads_set, 1)
            pool.memset(lamw[:, :], 1.0).then_inc(eps_set, 1)
            pool.wait_ge(cst_loaded, 16)
            for w, name in enumerate(("k1_b", "k2_b")):
                for m, mask in enumerate(("even", "odd")):
                    pool.tensor_tensor(kb[:, 2 * w + m:2 * w + m + 1], C(name), C(mask), ALU.mult).then_inc(kb_ready, 1)
            pool.wait_ge(neglam_ready, 2)
            pool.wait_ge(eps_set, 3)
            lv = lamw[:, :].rearrange("p (r g b m) -> p r g b m", r=4, g=4, b=2)
            nl = neglam[:, H:2 * H].rearrange("p (r m) -> p r m", m=2)
            for g in range(4):
                pool.tensor_copy(lv[:, :, g, 1, :], nl).then_inc(lamw_ready, 1)
            pool.wait_ge(conv_done, NSTEP)
            for b in range(2):
                pool.memset(qT[b][:, NTOK:NTOK + PAD], 0.0).then_inc(pads_set, 1)
            pool.memset(prob[:, :, :, :, :], 0.0).then_inc(probs_zeroed, 1)
            pool.wait_ge(probs_zeroed, 1)
            pool.wait_ge(lamw_ready, 4)
            for u in range(16):
                n, r = u // 4, u % 4
                c = slice(16 * r, 16 * r + 16)
                pool.wait_ge(rec_done, u + 1)
                if u >= 4:
                    pool.wait_ge(scaled, u - 3)
                pool.tensor_tensor(wr[:, c], rec[:, c], lamw[:, c], ALU.mult).then_inc(wr_done, 1)
                pool.wait_ge(wr_done, u + 1)
                ev = E[:, r, :].rearrange("p (x k) -> p x k", k=NS)
                pool.tensor_tensor(ev, ev, wr[:, c].unsqueeze(2).to_broadcast([P, 16, NS]), ALU.mult).then_inc(scaled, 1)
                pool.wait_ge(scaled, u + 1)
                if n >= 2:
                    pool.wait_ge(probT_done, n - 1)
                e4 = E[:, r, :].rearrange("p (g b m k) -> p g b m k", g=4, b=2, k=NS)
                for m in range(2):
                    pool.tensor_tensor(prob[:, n % 2, :, 2 * r + m, 0:NS], e4[:, :, 0, m, :], e4[:, :, 1, m, :],
                                       ALU.add).then_inc(prob_done, 1)
            pool.wait_ge(trans_done[1], NSTEP)
            pool.wait_ge(lnaff_ready, 1)
            for p, a, b in ((P, 0, NTILE - 1), (NTOK - (NTILE - 1) * TM, NTILE - 1, NTILE)):
                v = t6[0:p, a * TM:b * TM].rearrange("p (t d) -> p t d", d=D)
                pool.tensor_tensor(v, v, lnaff[0:p, D:2 * D].unsqueeze(1).to_broadcast([p, b - a, D]), ALU.add).then_inc(x2b_ready, 1)

        @block.scalar
        def _(act):
            def ln_sd(L, s, eps):
                n, rows, nt = step_tokens(s)
                act.wait_ge(aggr_done[L], 2 * s + nt)
                v = mv[L][0:rows, :].rearrange("p (t x) -> p t x", x=2)[:, 2 * s:2 * s + nt, 1]
                act.activation(sd[L][0:rows, 2 * s:2 * s + nt], v, ACT.Sqrt, bias=epsc[0:rows, eps:eps + 1]).then_inc(sd_done[L], 1)

            act.wait_ge(eps_set, 2)

            def z_evac(s):
                n = step_tokens(s)[0]
                act.wait_ge(trans_done[0], s + 1)
                act.activation(t1[:, s * ST:s * ST + n], PS[:, s, 0:n], ACT.Identity, bias=C("beta"), scale=C("gamma")).then_inc(z_ready, 1)

            for s in range(NSTEP):
                ln_sd(0, s, 0)
                if s == 0:
                    act.wait_ge(cst_loaded, 16)
                if s >= 2:
                    z_evac(s - 2)
            z_evac(NSTEP - 2)
            z_evac(NSTEP - 1)
            for c in range(NQ):
                act.wait_ge(dense_done, c + 1)
                act.activation(t2[:, c * QT:(c + 1) * QT], PS[:, c, 0:QT], ACT.Identity, bias=C("dense_b")).then_inc(h_ready, 1)
            act.wait_ge(kb_ready, 4)
            for c in range(NQ):
                act.wait_ge(proj_done[0], c + 1)
                act.activation(qT[0][:, c * QT:(c + 1) * QT], PS[:, 4, 0:QT], ACT.Copy).then_inc(proj_ready[0], 1)
                act.wait_ge(proj_done[3], c + 1)
                src = PS[:, 7, 0:QT].rearrange("p (b k) -> p b k", k=NS)
                for m, mask in enumerate(("even", "odd")):
                    act.activation(kX[1][:, c * QI:(c + 1) * QI, m, :], src, ACT.Identity,
                                   bias=kb[:, 2 + m:3 + m], scale=C(mask)).then_inc(proj_ready[3], 1)
            for v in (0, 2):
                act.wait_ge(v_done, v + 1)
                act.activation(vtok[:, 4 * v:4 * v + 4, :], PS[:, 4 + v, :].rearrange("p (g c) -> p g c", g=4), ACT.Copy).then_inc(v_ready[0], 1)
            act.wait_ge(lprod_ready, 2)
            act.activation(lexp[:, :], lprod[:, :], ACT.Exp).then_inc(lexp_ready, 1)

            def o_part(n):
                act.wait_ge(pv_done, n + 1)
                if n >= 1:
                    act.wait_ge(o_ready, 4 * n)
                src = PS[:, 4:8, 0:4 * 2 * NS].rearrange("p i (g m q) -> p i g m q", g=4, m=2)[:, :, :, 0, :]
                act.activation(otmp, src, ACT.Copy, scale=C("even")).then_inc(otmp_done, 1)

            for u in range(16):
                act.wait_ge(shifted, u + 1)
                act.activation(E[:, u % 4, :], E[:, u % 4, :], ACT.Exp, scale=HD ** -0.5).then_inc(exp_done, 1)
                if u % 4 == 3 and u >= 4:
                    o_part(u // 4 - 1)
            act.wait_ge(obias_ready, 1)
            act.wait_ge(v_done, NQ)
            act.activation(t2[:, 0:NTOK], t2[:, 0:NTOK], ACT.Identity, bias=obias[:, :]).then_inc(hb_ready, 1)
            o_part(3)
            for hf in range(2):
                c = slice(hf * NTOK // 2, (hf + 1) * NTOK // 2)
                act.wait_ge(gcent_done, hf + 1)
                act.activation(t5[:, c], t4[:, c], ACT.Square).then_inc(gsq_done, 1)
            for hf in range(2):
                b = slice(hf * NI // 2, (hf + 1) * NI // 2)
                act.wait_ge(gvar_done, hf + 1)
                act.activation(gns[:, 2, b], PS[:, 2 * hf + 1, 0:NI // 2], ACT.Sqrt, bias=epsc[:, 1:2]).then_inc(gsd_done, 1)

            def x2_evac(s):
                n = step_tokens(s)[0]
                act.wait_ge(trans_done[1], s + 1)
                act.activation(t3[:, s * ST:s * ST + n], PS[:, bank2[s], 0:n], ACT.Copy).then_inc(x2_ready, 1)
            for s in range(NSTEP):
                ln_sd(1, s, 1)
                if s >= 2:
                    x2_evac(s - 2)
            x2_evac(NSTEP - 2)
            x2_evac(NSTEP - 1)
            for c in range(NQ):
                act.wait_ge(gfc1_done, c + 1)
                act.activation(t5[:, c * QT:(c + 1) * QT], PS[:, 3 + c, 0:QT], ACT.Relu, bias=C("gfc1_b")).then_inc(gh_ready, 1)
            for m in range(1, 64, 2):
                cc = m // 8
                act.wait_ge(merge_done, m + 1)
                if m % 8 == 1 and cc >= 2:
                    weights_free(act, cc)
                evac_merged(act, m).then_inc(merged[1], 1)
            for s in range(NSTEP):
                ln_sd(2, s, 1)
                if s >= 1:
                    ln_sd(3, s - 1, 1)
            ln_sd(3, NSTEP - 1, 1)

        @block.vector
        def _(dve):
            for i in range(2):
                k = slice(i * KT // 2, (i + 1) * KT // 2)
                dve.wait_ge(w_loaded[i], 16)
                v = w5.rearrange("p (k g d) -> p k d g", k=KT, g=NSH)[:, k]
                dve.tensor_reduce(weff[:, k, :], v, AX.X, ALU.add).then_inc(weff_ready, 1)

            def ln_stats(L, s, src):
                n, rows, nt = step_tokens(s)
                for t in range(nt):
                    i = 2 * s + t
                    dve.bn_stats(st[L][0:rows, 6 * i:6 * i + 6], src(t, rows)).then_inc(stats_done[L], 1)
                for t in range(nt):
                    i = 2 * s + t
                    dve.wait_ge(stats_done[L], i + 1)
                    dve.bn_aggr(mv[L][0:rows, 2 * i:2 * i + 2], st[L][0:rows, 6 * i:6 * i + 6]).then_inc(aggr_done[L], 1)

            def ln_norm(L, s, src, dst):
                n, rows, nt = step_tokens(s)
                dve.wait_ge(sd_done[L], s + 1)
                dve.reciprocal(rs[L][0:rows, 2 * s:2 * s + nt], sd[L][0:rows, 2 * s:2 * s + nt]).then_inc(rstd_done[L], 1)
                dve.wait_ge(rstd_done[L], s + 1)
                for t in range(nt):
                    i = 2 * s + t
                    dve.tensor_scalar(dst[0:rows, i * TM:(i + 1) * TM], src(t, rows), mv[L][0:rows, 2 * i:2 * i + 1],
                                      rs[L][0:rows, i:i + 1], ALU.subtract, ALU.mult).then_inc(norm_done[L], 1)

            def bank_tile(b):
                return lambda t, rows: PS[0:rows, b, t * TM:(t + 1) * TM]

            for s in range(NSTEP + 1):
                if s < NSTEP:
                    dve.wait_ge(conv_done, s + 1)
                    ln_stats(0, s, bank_tile(s))
                if s >= 1:
                    ln_norm(0, s - 1, bank_tile(s - 1), t6)
            dve.wait_ge(cst_loaded, 16)
            lam = C("lam")
            for i in range(2):
                dve.tensor_tensor(lprod[:, i * H:(i + 1) * H], lam[:, 2 * i * H:(2 * i + 1) * H],
                                  lam[:, (2 * i + 1) * H:(2 * i + 2) * H], ALU.mult).then_inc(lprod_ready, 1)
            dve.wait_ge(small_done, 1)
            dve.tensor_scalar(obias[:, :], PS[:, 7, 0:1], C("out_b"), None, ALU.add).then_inc(obias_ready, 1)
            dve.tensor_copy(lnaff[:, :], PS[:, 7, 128:128 + 2 * D]).then_inc(lnaff_ready, 1)
            dve.wait_ge(kb_ready, 4)
            for c in range(NQ):
                dve.wait_ge(proj_done[1], c + 1)
                src = PS[:, 5, 0:QT].rearrange("p (b k) -> p b k", k=NS)
                for m, mask in enumerate(("even", "odd")):
                    dve.tensor_scalar(kX[0][:, c * QI:(c + 1) * QI, m, :], src, C(mask), kb[:, m:m + 1],
                                      ALU.mult, ALU.add).then_inc(proj_ready[1], 1)
                dve.wait_ge(proj_done[2], c + 1)
                dve.tensor_copy(qT[1][:, c * QT:(c + 1) * QT], PS[:, 6, 0:QT]).then_inc(proj_ready[2], 1)
            for v in (1, 3):
                dve.wait_ge(v_done, v + 1)
                dve.tensor_copy(vtok[:, 4 * v:4 * v + 4, :], PS[:, 4 + v, :].rearrange("p (g c) -> p g c", g=4)).then_inc(v_ready[1], 1)
            dve.wait_ge(lexp_ready, 1)
            dve.tensor_tensor(neglam[:, 0:H], lexp[:, H:2 * H], lexp[:, 0:H], ALU.subtract).then_inc(neglam_ready, 1)
            dve.wait_ge(neglam_ready, 1)
            dve.tensor_scalar(neglam[:, H:2 * H], neglam[:, 0:H], -0.2, None, ALU.add).then_inc(neglam_ready, 1)

            def soft_shift(u):
                n, r = u // 4, u % 4
                c = slice(16 * r, 16 * r + 16)
                src = PS[:, r, 0:UC].rearrange("p (x k) -> p x k", k=NS)
                dve.wait_ge(scores_done, u + 1)
                dve.tensor_reduce(mx[:, c], src, AX.X, ALU.max).then_inc(max_done, 1)
                dve.wait_ge(max_done, u + 1)
                if n >= 1:
                    dve.wait_ge(prob_done, 2 * (u - 3))
                dve.tensor_tensor(E[:, r, :].rearrange("p (x k) -> p x k", k=NS), src,
                                  mx[:, c].unsqueeze(2).to_broadcast([P, 16, NS]), ALU.subtract).then_inc(shifted, 1)

            def soft_sum(u):
                r = u % 4
                c = slice(16 * r, 16 * r + 16)
                dve.wait_ge(exp_done, u + 1)
                dve.tensor_reduce(sm[:, c], E[:, r, :].rearrange("p (x k) -> p x k", k=NS), AX.X, ALU.add).then_inc(sum_done, 1)
                dve.wait_ge(sum_done, u + 1)
                if u >= 4:
                    dve.wait_ge(wr_done, u - 3)
                dve.reciprocal(rec[:, c], sm[:, c]).then_inc(rec_done, 1)

            def prob_transpose(n):
                dve.wait_ge(prob_done, 8 * (n + 1))
                if n >= 2:
                    dve.wait_ge(pv_done, n - 1)
                dve.transpose(probT[:, n % 2].rearrange("p g h q -> p (g h q)"),
                              prob[:, n % 2].rearrange("p g h k -> p (g h k)")).then_inc(probT_done, 1)

            oT = t1[:, 0:NTOK].rearrange("p (n g i q) -> p n i g q", n=NQ, g=4, i=4)

            def o_sum(n):
                dve.wait_ge(otmp_done, n + 1)
                for i in range(4):
                    src = PS[:, 4 + i, 0:4 * 2 * NS].rearrange("p (g m q) -> p g m q", g=4, m=2)[:, :, 1, :]
                    dve.scalar_tensor_tensor(out=oT[:, n, i], in0=src, scalar=C("odd"), in1=otmp[:, i],
                                             op0=ALU.mult, op1=ALU.add).then_inc(o_ready, 1)

            for u in range(16 + 2):
                if u < 16:
                    soft_shift(u)
                if 1 <= u <= 16:
                    soft_sum(u - 1)
                if u % 4 == 1 and u > 4:
                    prob_transpose(u // 4 - 1)
                    if u > 8:
                        o_sum(u // 4 - 2)
            o_sum(3)

            HT, HI = NTOK // 2, NI // 2
            dve.wait_ge(o_ready, 16)
            for hf in range(2):
                b = slice(hf * HI, (hf + 1) * HI)
                dve.tensor_reduce(gns[:, 0, b], t1[:, hf * HT:(hf + 1) * HT].rearrange("p (b k) -> p b k", k=NS),
                                  AX.X, ALU.add).then_inc(gsum_done, 1)
            for hf in range(2):
                dve.wait_ge(gmean_done, hf + 1)
                dve.tensor_tensor(t4[:, hf * HT:(hf + 1) * HT].rearrange("p (b k) -> p b k", k=NS),
                                  t1[:, hf * HT:(hf + 1) * HT].rearrange("p (b k) -> p b k", k=NS),
                                  PS[:, 2 * hf, 0:HI].unsqueeze(2).to_broadcast([P, HI, NS]), ALU.subtract).then_inc(gcent_done, 1)
            for hf in range(2):
                b = slice(hf * HI, (hf + 1) * HI)
                dve.wait_ge(gsq_done, hf + 1)
                dve.tensor_reduce(gns[:, 1, b], t5[:, hf * HT:(hf + 1) * HT].rearrange("p (b k) -> p b k", k=NS),
                                  AX.X, ALU.add).then_inc(gsqsum_done, 1)
            dve.wait_ge(gcent_done, 2)
            for hf in range(2):
                b = slice(hf * HI, (hf + 1) * HI)
                dve.wait_ge(gsd_done, hf + 1)
                dve.reciprocal(gns[:, 3, b], gns[:, 2, b]).then_inc(grstd_done, 1)
                dve.wait_ge(grstd_done, hf + 1)
                v = t4[:, hf * HT:(hf + 1) * HT].rearrange("p (b k) -> p b k", k=NS)
                dve.scalar_tensor_tensor(out=v, in0=v, scalar=C("gn_w"), in1=gns[:, 3, b].unsqueeze(2).to_broadcast([P, HI, NS]),
                                         op0=ALU.mult, op1=ALU.mult).then_inc(xn_ready, 1)

            for s in range(NSTEP + 1):
                if s < NSTEP:
                    dve.wait_ge(attn_done, s + 1)
                    ln_stats(1, s, bank_tile(bank2[s]))
                if s >= 1:
                    ln_norm(1, s - 1, bank_tile(bank2[s - 1]), t6)
            for c in range(NQ):
                dve.wait_ge(gh_ready, c + 1)
                dve.tensor_reduce(ghsum[:, c * QI:(c + 1) * QI], t5[:, c * QT:(c + 1) * QT].rearrange("p (b k) -> p b k", k=NS),
                                  AX.X, ALU.add).then_inc(ghsum_done, 1)
            dve.wait_ge(gfc2_done, 1)
            dve.tensor_scalar(gate1, PS[0:R, 7, 0:NI], 1.0 / NS, C("gate_b", R), ALU.mult, ALU.add).then_inc(gate1_done, 1)
            dve.wait_ge(gate1_done, 1)
            dve.tensor_tensor(gates, gate1.unsqueeze(1).to_broadcast([R, NJ, NI]),
                              C("slice", R).unsqueeze(2).to_broadcast([R, NJ, NI]), ALU.mult).then_inc(gates_ready, 1)
            dve.wait_ge(b1_done, 1)
            b1v = PS[:, 3, 0:NC * NI].rearrange("p (c b) -> p c b", c=NC)
            dve.tensor_scalar(nb1, b1v, -1.0, None, ALU.mult).then_inc(b1_ready, 1)
            dve.tensor_copy(hidv[:, :, :, NS], b1v).then_inc(b1col_ready, 1)
            dve.wait_ge(b1_ready, 1)

            def hidden(c):
                for q in range(NQ):
                    dve.wait_ge(pre_done, NQ * c + q + 1)
                    dve.tensor_tensor(hidv[:, c, q * QI:(q + 1) * QI, 0:NS], PS[:, 4 + q, 0:QT].rearrange("p (b k) -> p b k", k=NS),
                                      nb1[:, c, q * QI:(q + 1) * QI].unsqueeze(2).to_broadcast([P, QI, NS]), ALU.max).then_inc(hid_ready, 1)

            for cc in range(2 * NC + 1):
                if cc < 2 * NC:
                    for m in range(8 * cc, 8 * cc + 8, 2):
                        dve.wait_ge(merge_done, m + 1)
                        if m % 8 == 0 and cc >= 2:
                            weights_free(dve, cc)
                        evac_merged(dve, m).then_inc(merged[0], 1)
                if 1 <= cc <= NC:
                    hidden(cc - 1)

            for q in range(NQ):
                v = PS[:, 4 + q, 0:QI * HC].rearrange("p (b k) -> p b k", k=HC)
                dve.wait_ge(ffn_done, q + 1)
                rq = t1[:, q * QT:(q + 1) * QT].rearrange("p (b k) -> p b k", k=NS)
                dve.tensor_tensor(rq, v[:, :, 0:NS], t3[:, q * QT:(q + 1) * QT].rearrange("p (b k) -> p b k", k=NS),
                                  ALU.add).then_inc(res_part, 1)
                dve.wait_ge(res_part, q + 1)
                dve.tensor_tensor(rq, rq, v[:, :, NS:HC].to_broadcast([P, QI, NS]), ALU.add).then_inc(res_ready, 1)

            dve.wait_ge(x2b_ready, 2)

            def affine(s):
                n, rows, nt = step_tokens(s)
                v = t4[0:rows, s * ST:s * ST + nt * TM]
                v3 = v.rearrange("p (t d) -> p t d", d=D)
                dve.wait_ge(norm_done[2], min(2 * s + nt, NTILE))
                dve.tensor_tensor(v3, v3, lnaff[0:rows, 0:D].unsqueeze(1).to_broadcast([rows, nt, D]), ALU.mult).then_inc(aff_part, 1)
                dve.wait_ge(aff_part, s + 1)
                dve.tensor_tensor(v, v, t6[0:rows, s * ST:s * ST + nt * TM], ALU.add).then_inc(aff_done, 1)

            def t4_tile(s):
                return lambda t, rows: t4[0:rows, s * ST + t * TM:s * ST + (t + 1) * TM]

            for s in range(NSTEP + 2):
                if s < NSTEP:
                    dve.wait_ge(trans_done[2], s + 1)
                    ln_stats(2, s, bank_tile(s))
                if 1 <= s <= NSTEP:
                    ln_norm(2, s - 1, bank_tile(s - 1), t4)
                    affine(s - 1)
                    dve.wait_ge(aff_done, s)
                    ln_stats(3, s - 1, t4_tile(s - 1))
                if s >= 2:
                    ln_norm(3, s - 2, t4_tile(s - 2), t5)

        @block.tensor
        def _(pe):
            def transposes(L, s, bank, src):
                n, rows, nt = step_tokens(s)
                pe.wait_ge(norm_done[L], min(2 * s + nt, NTILE))
                for t in range(nt):
                    i = 2 * s + t
                    mm = pe.transpose(PS[:, bank, t * TM:t * TM + rows], src[0:rows, i * TM:(i + 1) * TM], ident[0:rows, 0:rows])
                mm.then_inc(trans_done[L], 1)

            def conv(s):
                n, rows, nt = step_tokens(s)
                pe.wait_ge(x_loaded[s], 16)
                for t in range(nt):
                    for k in range(KT):
                        if s == 0 and t == 0 and k % (KT // 2) == 0:
                            pe.wait_ge(weff_ready, k // (KT // 2) + 1)
                        mm = pe.matmul(PS[0:rows, s, t * TM:(t + 1) * TM], xs(s)[:, k, t * TM:t * TM + rows], weff[:, k, :],
                                       start=(k == 0), stop=(k == KT - 1))
                mm.then_inc(conv_done, 1)

            for s in range(NSTEP):
                conv(s)
                if s == 1:
                    pe.wait_ge(cst_loaded, 16)
                if s >= 2:
                    transposes(0, s - 2, s - 2, t6)
            transposes(0, NSTEP - 2, NSTEP - 2, t6)
            transposes(0, NSTEP - 1, NSTEP - 1, t6)
            pe.matmul(PS[:, 7, 0:1], C("o"), C("gn_b"), start=True, stop=True)
            pe.matmul(PS[:, 7, 128:256], C("coef", NE + 1), C("ln_g", NE + 1), start=True, stop=True)
            pe.matmul(PS[:, 7, 256:384], C("coef", NE + 1), C("ln_b", NE + 1), start=True, stop=True).then_inc(small_done, 1)
            for c in range(NQ):
                pe.wait_ge(z_ready, steps_for[c])
                pe.matmul(PS[:, c, 0:QT], C("dense_w"), t1[:, c * QT:(c + 1) * QT], start=True, stop=True).then_inc(dense_done, 1)
            pe.wait_ge(z_ready, NSTEP)
            pe.wait_ge(obias_ready, 1)
            pe.wait_ge(lnaff_ready, 1)
            for c in range(NQ):
                pe.wait_ge(h_ready, c + 1)
                for w, name in enumerate(("q1", "k1", "q2", "k2")):
                    if c >= 1:
                        pe.wait_ge(proj_ready[w], (2 if w in (1, 3) else 1) * c)
                    pe.matmul(PS[:, 4 + w, 0:QT], C(name), t2[:, c * QT:(c + 1) * QT], start=True, stop=True).then_inc(proj_done[w], 1)
            pe.wait_ge(pads_set, 1)
            for v in range(4):
                pe.wait_ge(proj_ready[v], 2 * NQ if v in (1, 3) else NQ)
                for g in range(4):
                    for i in range(4):
                        c = ((4 * v + g) * 4 + i) * NS
                        mm = pe.matmul(PS[32 * i:32 * i + 32, 4 + v, g * D:(g + 1) * D], t2[:, c:c + 32], C("v"), start=True, stop=True)
                mm.then_inc(v_done, 1)

            def scores(u):
                n, r = u // 4, u % 4
                if n >= 1:
                    pe.wait_ge(shifted, u - 3)
                for g in range(4):
                    for b in range(2):
                        for i in range(4):
                            im = (n * 4 + g) * 4 + i
                            c = (g * 2 + b) * 2 * NS
                            mm = pe.matmul(PS[32 * i:32 * i + 32, r, c:c + 2 * NS],
                                           qT[b][32 * r:32 * r + 32, im * NS:im * NS + 32],
                                           kX[b][32 * r:32 * r + 32, im, :, :], start=True, stop=True)
                mm.then_inc(scores_done, 1)

            def values(n):
                pe.wait_ge(probT_done, n + 1)
                if n >= 1:
                    pe.wait_ge(o_ready, 4 * n)
                for i in range(4):
                    for g in range(4):
                        for r in range(4):
                            mm = pe.matmul(PS[32 * r:32 * r + 32, 4 + i, g * 2 * NS:(g + 1) * 2 * NS],
                                           vtok[32 * i:32 * i + 32, 4 * n + g, 32 * r:32 * r + 32],
                                           probT[32 * i:32 * i + 32, n % 2, g, 2 * r:2 * r + 2, 0:NS], start=True, stop=True)
                mm.then_inc(pv_done, 1)

            pe.wait_ge(pads_set, 3)
            pe.wait_ge(v_ready[0], 2)
            pe.wait_ge(v_ready[1], 2)
            for n in range(NQ):
                for r in range(4):
                    scores(4 * n + r)
                if n >= 1:
                    values(n - 1)
            values(NQ - 1)
            HI = NI // 2
            for hf in range(2):
                pe.wait_ge(gsum_done, hf + 1)
                pe.matmul(PS[:, 2 * hf, 0:HI], C("gnsum"), gns[:, 0, hf * HI:(hf + 1) * HI], start=True, stop=True).then_inc(gmean_done, 1)
            for hf in range(2):
                pe.wait_ge(gsqsum_done, hf + 1)
                pe.matmul(PS[:, 2 * hf + 1, 0:HI], C("gnsum"), gns[:, 1, hf * HI:(hf + 1) * HI], start=True, stop=True).then_inc(gvar_done, 1)
            pe.wait_ge(hb_ready, 1)
            for s in range(NSTEP):
                n, rows, nt = step_tokens(s)
                pe.wait_ge(xn_ready, 1 if (s + 1) * ST <= NTOK // 2 else 2)
                for t in range(nt):
                    c = slice(s * ST + t * TM, s * ST + t * TM + rows)
                    o = PS[0:rows, bank2[s], t * TM:(t + 1) * TM]
                    pe.matmul(o, t4[:, c], C("o"), start=True, stop=False)
                    mm = pe.matmul(o, t2[:, c], ident, start=False, stop=True)
                mm.then_inc(attn_done, 1)
                if s >= 2:
                    transposes(1, s - 2, bank2[s - 2], t6)
            transposes(1, NSTEP - 2, bank2[NSTEP - 2], t6)
            transposes(1, NSTEP - 1, bank2[NSTEP - 1], t6)
            for c in range(NQ):
                pe.wait_ge(x2_ready, steps_for[c])
                pe.matmul(PS[:, 3 + c, 0:QT], C("gfc1"), t3[:, c * QT:(c + 1) * QT], start=True, stop=True).then_inc(gfc1_done, 1)
            pe.wait_ge(ghsum_done, NQ)
            pe.matmul(PS[0:R, 7, 0:NI], C("gfc2"), ghsum, start=True, stop=True).then_inc(gfc2_done, 1)
            pe.wait_ge(gates_ready, 1)
            for c in range(NC):
                mm = pe.matmul(PS[:, 3, c * NI:(c + 1) * NI], C("tvb1", R)[:, c * P:(c + 1) * P], gates[:, 0, :], start=True, stop=True)
            mm.then_inc(b1_done, 1)

            def merge(cc):
                w = tvw[cc // NC][:, :].rearrange("p (c s m) -> p c s m", c=NC, m=P)
                if cc % NC == 0:
                    pe.wait_ge(tv_loaded[cc // NC], 16)
                for m in range(8 * cc, 8 * cc + 8):
                    if m >= 2:
                        pe.wait_ge(merged[m % 2], m // 2)
                    if m == 1:
                        pe.wait_ge(b1col_ready, 1)
                    for i in range(2):
                        mm = pe.matmul(PS[:, 2 * (m % 2) + i, :], w[:, cc % NC, 2 * (m % 8) + i, :], gates.rearrange("p j b -> p (j b)"),
                                       start=True, stop=True)
                    mm.then_inc(merge_done, 1)

            def apply1(c):
                pe.wait_ge(merged[0], 4 * (c + 1))
                pe.wait_ge(merged[1], 4 * (c + 1))
                for q in range(NQ):
                    if c >= 1:
                        pe.wait_ge(hid_ready, NQ * (c - 1) + q + 1)
                    for b in range(QI):
                        im = q * QI + b
                        mm = pe.matmul(PS[:, 4 + q, b * NS:(b + 1) * NS], wm[c % 2][:, im, :], t3[:, im * NS:(im + 1) * NS],
                                       start=True, stop=True)
                    mm.then_inc(pre_done, 1)

            def apply2(c):
                pe.wait_ge(merged[0], 4 * (NC + c + 1))
                pe.wait_ge(merged[1], 4 * (NC + c + 1))
                pe.wait_ge(hid_ready, NQ * NC)
                for q in range(NQ):
                    for b in range(QI):
                        im = q * QI + b
                        pe_mm = pe.matmul(PS[:, 4 + q, b * HC:(b + 1) * HC], wm[c % 2][:, im, :], hidv[:, c, im, :],
                                          start=(c == 0 and b == 0), stop=(c == NC - 1), skip_group_check=True)
                    if c == NC - 1:
                        col = PS[:, 4 + q, 0:QI * HC].rearrange("p (b k) -> p b k", k=HC)[:, :, NS]
                        pe.matmul(col, C("tvb2", R), gates[:, 0, q * QI:(q + 1) * QI], start=False, stop=True,
                                  skip_group_check=True).then_inc(ffn_done, 1)
                if c < NC - 1:
                    pe_mm.then_inc(applied, 1)

            def apply(cc):
                apply1(cc) if cc < NC else apply2(cc - NC)

            merge(0)
            for cc in range(1, 2 * NC):
                merge(cc)
                apply(cc - 1)
            apply(2 * NC - 1)
            for s in range(NSTEP):
                n, rows, nt = step_tokens(s)
                pe.wait_ge(res_ready, res_for[s])
                for t in range(nt):
                    c = slice(s * ST + t * TM, s * ST + t * TM + rows)
                    mm = pe.transpose(PS[0:rows, s, t * TM:(t + 1) * TM], t1[:, c], ident)
                mm.then_inc(trans_done[2], 1)



def _layout(np, i):
    f4 = np.float32
    a = {k: np.asarray(v) for k, v in i.items()}
    x = a["x"]
    xp = np.zeros((NI, x.shape[1] + 1, x.shape[2] + 1, 3), f4)
    xp[:, 1:, 1:] = x
    win = np.zeros((NI, 5, 5, 18, 18, 3), f4)
    for r in range(5):
        for c in range(5):
            win[:, r, c] = xp[:, 16 * r:16 * r + 18, 16 * c:16 * c + 18]
    k = 18 * 18 * 3
    xcol = np.zeros((KT * P, NTOK), f4)
    xcol[:k] = win.reshape(NTOK, k).T
    xcol[k] = 1.0
    xcol = xcol.reshape(KT, P, NTOK).transpose(1, 0, 2)
    parts = []
    for s in range(NSTEP):
        n = step_tokens(s)[0]
        parts.append(xcol[:, :, s * ST:s * ST + n].reshape(P, KT * n))
    w = a["L0_tok_conv_w"].reshape(16, 16, NSH, 3, D)
    w5 = np.zeros((18, 18, 3, NSH, D), f4)
    for g, (r, c) in enumerate(((1, 1), (1, 0), (1, 2), (0, 1), (2, 1))):
        w5[r:r + 16, c:c + 16, :, g] = w[:, :, g]
    wc = np.zeros((KT * P, NSH, D), f4)
    wc[:k] = w5.reshape(k, NSH, D)
    wc[k, 0] = a["L0_tok_conv_b"]
    wc = wc.reshape(KT, P, NSH * D).transpose(1, 0, 2).reshape(P, KT * NSH * D)

    cst = np.zeros((P, NCONST), f4)

    def put(name, v):
        lo, hi = COL[name]
        v = v.reshape(v.shape[0], -1)
        assert v.shape[1] == hi - lo, name
        cst[0:v.shape[0], lo:hi] = v
    put("dense_w", a["L0_tok_dense_w"])
    for name, src in (("q1", "Q1"), ("k1", "K1"), ("q2", "Q2"), ("k2", "K2"), ("v", "V"), ("o", "out")):
        put(name, a[f"L0_attn_{src}_w"].T)
    put("gfc1", a["L0_ffn_gfc1_w"].T)
    put("gfc2", np.repeat(np.concatenate([np.zeros((1, D), f4), a["L0_ffn_gfc2_w"]]), NJ, 0).T)
    for name, src in (("gamma", "tok_gamma"), ("beta", "tok_beta"), ("dense_b", "tok_dense_b"), ("k1_b", "attn_K1_b"),
                      ("k2_b", "attn_K2_b"), ("gn_w", "attn_gn_w"), ("gn_b", "attn_gn_b"), ("out_b", "attn_out_b"),
                      ("gfc1_b", "ffn_gfc1_b")):
        put(name, a["L0_" + src].reshape(P, 1))
    put("gate_b", np.repeat(np.concatenate([np.ones(1, f4), a["L0_ffn_gfc2_b"]]), NJ).reshape(R, 1))
    p = np.arange(P)
    put("even", (p // HD % 2 == 0).astype(f4).reshape(P, 1))
    put("odd", (p // HD % 2 == 1).astype(f4).reshape(P, 1))
    put("slice", np.tile(np.eye(NJ, dtype=f4), (NE + 1, 1)))
    put("tvb1", np.repeat(np.concatenate([a["L0_ffn_b1"][None], a["L0_ffn_tv_b1"]]), NJ, 0))
    put("tvb2", np.repeat(np.concatenate([a["L0_ffn_b2"][None], a["L0_ffn_tv_b2"]]), NJ, 0))
    put("ln_g", np.concatenate([a["L0_ffn_ln_g"][None], a["L0_ffn_tv_ln_g"]]))
    put("ln_b", np.concatenate([a["L0_ffn_ln_b"][None], a["L0_ffn_tv_ln_b"]]))
    coef = np.full((NE + 1, P), 0.03, f4)
    coef[0] = 1 - 0.03 * NE
    put("coef", coef)
    put("gnsum", (p[:, None] // 32 == p[None] // 32).astype(f4) / (32 * NS))
    put("ident", np.eye(P, dtype=f4))
    lam = np.concatenate([a["L0_attn_lambda_" + n].reshape(-1) for n in ("q1", "k1", "q2", "k2")])
    put("lam", np.broadcast_to(lam, (P, 4 * H)))

    w1 = np.concatenate([a["L0_ffn_W1"][None], a["L0_ffn_tv_W1"]]).reshape(NE + 1, NC, NJ, SJ, D)
    w2 = np.concatenate([a["L0_ffn_W2"][None], a["L0_ffn_tv_W2"]]).reshape(NE + 1, NJ, SJ, NC, P)
    return {
        "consts": cst, "conv_filter": np.ascontiguousarray(wc), "windows": np.concatenate(parts, 1),
        "tv_w1": np.ascontiguousarray(w1.transpose(0, 2, 1, 3, 4).reshape(R, NC * SJ * P)),
        "tv_w2": np.ascontiguousarray(w2.transpose(0, 1, 3, 2, 4).reshape(R, NC * SJ * P)),
    }


def kernel(**inputs):
    import numpy as _np
    import concourse.bacc as _bacc
    from concourse import mybir as _mybir
    from concourse.bass_utils import run_bass_kernel_spmd as _run

    arrays = _layout(_np, inputs)
    nc = _bacc.Bacc("TRN2", target_bir_lowering=False, num_devices=1)
    f32 = _mybir.dt.float32
    d = {n: nc.dram_tensor(n, v.shape, f32, kind="ExternalInput").ap() for n, v in arrays.items()}
    out = nc.dram_tensor("out", (NTOK, D), f32, kind="ExternalOutput").ap()
    cols = [KT * ST * s for s in range(NSTEP)] + [KT * NTOK]
    xcol = [d["windows"][:, cols[s]:cols[s + 1]].rearrange("p (k n) -> p k n", k=KT) for s in range(NSTEP)]
    build(nc, d["consts"], d["conv_filter"], xcol, d["tv_w1"], d["tv_w2"], out)
    r = _run(nc, [arrays], core_ids=[0])
    return r.results[0]["out"].reshape(NI, NS, D)
```

```python
import concourse.bass as bass
from concourse import mybir
from contextlib import ExitStack

P = 128
NI, NS = 64, 25
NTOK = NI * NS
D, H, HD = 128, 8, 16
F, NE = 512, 8
KT = 8
NSH = 5
TM = 128
ST = 2 * TM
NSTEP = -(-NTOK // ST)
NTILE = -(-NTOK // TM)
NQ = 4
QI, QT = NI // NQ, NTOK // NQ
NG = NI // 4
NC = F // P
PAD = 8
TP = NTOK + PAD
NPS = NG // 2

NJ = 2
SJ = P // NJ
TERMS = [(0, 0), (0, 1), (0, 2), (1, 0), (1, 1), (2, 0)]
RE = NE * NJ
RB = len(TERMS) * RE
R = RB + 3 * NJ
WROW = NC * SJ * P
NU = P // RE
HE, HB = WROW // NU // 2, NJ * WROW // P // 2
HS = HE + HB

_COLS = [("dense_w", 128), ("q1", 128), ("k1", 128), ("q2", 128), ("k2", 128), ("v", 128), ("o", 128),
         ("gfc1", 128), ("gfc2", R), ("gpart", 3), ("gamma", 1), ("beta", 1), ("dense_b", 1), ("k1_b", 1), ("k2_b", 1),
         ("gn_w", 1), ("gn_b", 1), ("out_b", 1), ("gfc1_b", 1), ("gate_b", 1), ("even", 1), ("odd", 1),
         ("slice", NJ), ("tvb1", F), ("tvb2", D), ("ln_g", D), ("ln_b", D), ("coef", 128),
         ("gnsum", 128), ("ident", 128), ("lam", 4 * H)]
COL, _at = {}, 0
for _n, _w in _COLS:
    COL[_n] = (_at, _at + _w)
    _at += _w
NCONST = _at


def step_tokens(s):
    n = min(ST, NTOK - s * ST)
    return n, min(n, TM), -(-n // TM)


def build(nc, cst_d, wconv_d, xcol_d, tvw_d, sce_d, scb_d, out_d):
    f32 = mybir.dt.float32
    bf16 = mybir.dt.bfloat16
    ALU = mybir.AluOpType
    ACT = mybir.ActivationFunctionType
    AX = mybir.AxisListType
    ctx = ExitStack()
    with ctx:
        def sb(name, cols, rows=P, dt=f32):
            return ctx.enter_context(nc.sbuf_tensor(name, [rows, cols], dt))

        def sem(name):
            return ctx.enter_context(nc.semaphore(name))

        cst = sb("cst", NCONST)
        arena = sb("arena", 2 * NI * P)
        hid = sb("hid", NC * TP)
        wrow = sb("wrow", 2 * SJ * P, R, bf16)
        stage = sb("stage", HS)
        part = [sb(f"part{i}", HS, P, bf16) for i in range(3)]
        t1 = sb("t1", NG * P)
        t2 = sb("t2", TP)
        t3 = sb("t3", TP)
        t4 = sb("t4", NG * P)
        t5 = sb("t5", NG * P)
        t6 = sb("t6", NG * P)
        PS = ctx.enter_context(nc.psum_tensor("PS", [P, 8, 512], f32))

        def C(name, rows=P):
            a, b = COL[name]
            return cst[0:rows, a:b]

        def xs(s):
            n = step_tokens(s)[0]
            return arena[:, KT * ST * s:KT * ST * s + KT * n].rearrange("p (k n) -> p k n", k=KT)

        w5 = hid[:, 0:KT * NSH * D]
        weff = hid[:, KT * NSH * D:KT * (NSH + 1) * D].rearrange("p (k d) -> p k d", k=KT)
        at = [0]

        def take(n):
            at[0] += n
            assert at[0] <= 2 * NI * P
            return arena[:, at[0] - n:at[0]]
        qT = [take(NTOK + PAD) for _ in range(2)]
        kX = [take(2 * NTOK).rearrange("p (b m k) -> p b m k", m=2, k=NS) for _ in range(2)]
        vtok = take(NG * D).rearrange("p (g c) -> p g c", g=NG)
        UC = 4 * 2 * 2 * NS
        E = take(4 * UC).rearrange("p (u c) -> p u c", u=4)
        prob = take(2 * 4 * H * 32).rearrange("p (n g h k) -> p n g h k", n=2, g=4, h=H)
        probT = hid[:, 0:2 * 4 * H * 32].rearrange("p (n g h q) -> p n g h q", n=2, g=4, h=H)
        otmp = hid[:, 2048:2048 + QT].rearrange("p (i g q) -> p i g q", i=4, g=4)
        gns = hid[:, 3000:3000 + 4 * NI].rearrange("p (a b) -> p a b", a=4)
        wm = [arena[:, i * NI * P:(i + 1) * NI * P].rearrange("p (b m) -> p b m", b=NI) for i in range(2)]
        hidv = hid[:, :].rearrange("p (c n) -> p c n", c=NC)
        b1m = t4[:, 0:NC * NI].rearrange("p (c b) -> p c b", c=NC)
        gate1 = t4[0:R, 256:256 + NI]
        grest = t4[0:R, 320:320 + NI]
        gsel = t4[0:R, 384:384 + NI]
        ghsum = t4[:, 448:448 + NI]
        gtok = t5[0:R, 0:NI * 32].rearrange("p (b q) -> p b q", b=NI)
        gpart = [sb(f"gpart{i}", NI, R, bf16) for i in range(3)]
        gates = sb("gates", NJ * NI, R, bf16)

        mx = sb("mx", 64)
        sm = sb("sm", 64)
        rec = sb("rec", 64)
        wr = sb("wr", 64)
        lamw = sb("lamw", 64)
        lprod = sb("lprod", 2 * H)
        lexp = sb("lexp", 2 * H)
        neglam = sb("neglam", 2 * H)
        kb = sb("kb", 4)
        epsc = sb("epsc", 2)
        obias = sb("obias", 1)
        lnaff = sb("lnaff", 2 * D)
        nms = sb("nms", NG)
        st = [sb(f"st{i}", NG * 6) for i in range(4)]
        mv = [sb(f"mv{i}", NG * 2) for i in range(4)]
        sd = [sb(f"sd{i}", NG) for i in range(4)]
        rs = [sb(f"rs{i}", NG) for i in range(4)]

        w_loaded = [sem(f"w_loaded{i}") for i in range(2)]
        x_loaded = [sem(f"x_loaded{i}") for i in range(NSTEP)]
        cst_loaded = sem("cst_loaded")
        stage_loaded = [sem(f"stage_loaded{i}") for i in range(4)]
        part_done = [sem(f"part_done{i}") for i in range(3)]
        rest_done = sem("rest_done")
        scratch_written = [sem(f"scratch_written{i}") for i in range(4)]
        wrow_loaded = [sem(f"wrow_loaded{i}") for i in range(2)]
        stored = sem("stored")
        weff_ready = sem("weff_ready")
        conv_done = sem("conv_done")
        eps_set = sem("eps_set")
        stats_done = [sem(f"stats_done{i}") for i in range(4)]
        aggr_done = [sem(f"aggr_done{i}") for i in range(4)]
        sd_done = [sem(f"sd_done{i}") for i in range(4)]
        rstd_done = [sem(f"rstd_done{i}") for i in range(4)]
        norm_done = [sem(f"norm_done{i}") for i in range(4)]
        trans_done = [sem(f"trans_done{i}") for i in range(3)]
        z_ready = sem("z_ready")
        dense_done = sem("dense_done")
        h_ready = sem("h_ready")
        small_done = sem("small_done")
        obias_ready = sem("obias_ready")
        lnaff_ready = sem("lnaff_ready")
        kb_ready = sem("kb_ready")
        pads_set = sem("pads_set")
        probs_zeroed = sem("probs_zeroed")
        proj_done = [sem(f"proj_done{w}") for w in range(4)]
        proj_ready = [sem(f"proj_ready{w}") for w in range(4)]
        v_done = sem("v_done")
        v_ready = [sem("v_ready_act"), sem("v_ready_dve")]
        lprod_ready = sem("lprod_ready")
        lexp_ready = sem("lexp_ready")
        neglam_ready = sem("neglam_ready")
        lamw_ready = sem("lamw_ready")
        hb_ready = sem("hb_ready")
        scores_done = sem("scores_done")
        max_done = sem("max_done")
        shifted = sem("shifted")
        exp_done = sem("exp_done")
        sum_done = sem("sum_done")
        rec_done = sem("rec_done")
        wr_done = sem("wr_done")
        scaled = sem("scaled")
        prob_done = sem("prob_done")
        probT_done = sem("probT_done")
        pv_done = sem("pv_done")
        otmp_done = sem("otmp_done")
        o_ready = sem("o_ready")
        gsum_done = sem("gsum_done")
        gmean_done = sem("gmean_done")
        gcent_done = sem("gcent_done")
        gsq_done = sem("gsq_done")
        gsqsum_done = sem("gsqsum_done")
        gvar_done = sem("gvar_done")
        gsd_done = sem("gsd_done")
        grstd_done = sem("grstd_done")
        xn_ready = sem("xn_ready")
        attn_done = sem("attn_done")
        x2_ready = sem("x2_ready")
        gfc1_done = sem("gfc1_done")
        gh_ready = sem("gh_ready")
        ghsum_done = sem("ghsum_done")
        gfc2_done = sem("gfc2_done")
        gate1_done = sem("gate1_done")
        gsplit = sem("gsplit")
        gtok_done = sem("gtok_done")
        gates_ready = sem("gates_ready")
        b1_done = sem("b1_done")
        b1_ready = sem("b1_ready")
        merge_done = sem("merge_done")
        merged = [sem("merged_by_dve"), sem("merged_by_act")]
        applied = sem("applied")
        pre_done = sem("pre_done")
        htok_ready = sem("htok_ready")
        htrans_done = sem("htrans_done")
        biased = sem("biased")
        hid_ready = sem("hid_ready")
        ffn_done = sem("ffn_done")
        res_ready = sem("res_ready")
        x2b_ready = sem("x2b_ready")
        shift_done = sem("shift_done")
        aff_part = sem("aff_part")
        aff_done = sem("aff_done")

        ident = C("ident")
        steps_for = [-(-min(NTOK, QT * (c + 1)) // ST) for c in range(NQ)]
        bank2 = [4, 5, 6, 7, 0, 1, 2, 3]
        gbank = [bank2[2 * c] for c in range(NQ)]

        def tiles(L, s):
            if L == 0:
                n, rows, nt = step_tokens(s)
                return n, rows, nt, min(2 * s + nt, NTILE)
            return ST, P, 2, 2 * s + 2

        def merged_views(m):
            cc, k = m // 8, m % 8
            b0 = 2 * (m % 2)
            src = PS[:, b0:b0 + 2, :].rearrange("p n (s j b) -> p (n s) j b", j=NJ, b=NI)
            dst = wm[cc % 2].rearrange("p b (j s) -> p s j b", j=NJ)[:, 8 * k:8 * k + 8]
            return src, dst

        def weights_free(eng, cc):
            if cc - 2 < NC:
                eng.wait_ge(pre_done, NQ * (cc - 1))
            else:
                eng.wait_ge(applied, cc - 1 - NC)

        def evac_merged(eng, m):
            src, dst = merged_views(m)
            if m % 2:
                return eng.activation(dst, src, ACT.Copy)
            return eng.tensor_copy(dst, src)

        block = ctx.enter_context(nc.Block())

        @block.sync
        def _(sp):
            half = KT // 2 * NSH * D
            sp.dma_start(w5[:, 0:half], wconv_d[:, 0:half]).then_inc(w_loaded[0], 16)
            sp.dma_start(xs(0), xcol_d[0]).then_inc(x_loaded[0], 16)
            sp.dma_start(w5[:, half:2 * half], wconv_d[:, half:2 * half]).then_inc(w_loaded[1], 16)
            sp.dma_start(cst[:, :], cst_d).then_inc(cst_loaded, 16)
            for s in range(1, NSTEP):
                sp.dma_start(xs(s), xcol_d[s]).then_inc(x_loaded[s], 16)
            sp.dma_start(stage[:, :], tvw_d[0]).then_inc(stage_loaded[0], 16)

            def store_parts(h):
                m, hv = h // 2, h % 2
                for i in range(3):
                    sp.wait_ge(part_done[i], h + 1)
                    sp.dma_start(sce_d[m, i][:, hv * HE:(hv + 1) * HE], part[i][:, 0:HE]).then_inc(scratch_written[h], 16)
                    sp.dma_start(scb_d[m, i][:, hv * HB:(hv + 1) * HB], part[i][:, HE:HS]).then_inc(scratch_written[h], 16)
                if h < 3:
                    sp.dma_start(stage[:, :], tvw_d[h + 1]).then_inc(stage_loaded[h + 1], 16)

            def load_rows(cc):
                m, c, slot = cc // NC, cc % NC, cc % 2
                if cc >= 2:
                    sp.wait_ge(merge_done, 8 * (cc - 1))
                row = 0
                for i in range(3):
                    copies = sum(t[0] == i for t in TERMS)
                    src = sce_d[m, i].rearrange("(r u) n -> r (u n)", u=NU)[:, c * SJ * P:(c + 1) * SJ * P]
                    for _ in range(copies):
                        sp.dma_start(wrow[row:row + RE, slot * SJ * P:(slot + 1) * SJ * P], src).then_inc(wrow_loaded[slot], 16)
                        row += RE
                src = scb_d[m].rearrange("i (j u) n -> (i j) (u n)", j=NJ)[:, c * SJ * P:(c + 1) * SJ * P]
                sp.dma_start(wrow[RB:R, slot * SJ * P:(slot + 1) * SJ * P], src).then_inc(wrow_loaded[slot], 16)

            for m in range(2):
                store_parts(2 * m)
                store_parts(2 * m + 1)
                if m == 0:
                    for h in range(2):
                        sp.wait_ge(scratch_written[h], 16 * 6)
                    load_rows(0)
                    load_rows(1)
            for h in range(2, 4):
                sp.wait_ge(scratch_written[h], 16 * 6)
            for cc in range(2, 2 * NC):
                load_rows(cc)
            out_v = out_d.rearrange("(g i q) d -> i q g d", i=4, q=NS)
            for s in range(0, NPS, 2):
                sp.wait_ge(norm_done[3], 2 * (s + 2))
                for i in range(4):
                    src = t5[32 * i:32 * i + NS, s * ST:(s + 2) * ST].rearrange("p (g d) -> p g d", d=D)
                    sp.dma_start(out_v[i][:, 2 * s:2 * s + 4, :], src).then_inc(stored, 16)
            sp.wait_ge(stored, 16 * 4 * (NPS // 2))

        @block.gpsimd
        def _(pool):
            pool.memset(epsc[:, 0:1], 1e-3).then_inc(eps_set, 1)
            pool.memset(epsc[:, 1:2], 1e-5).then_inc(eps_set, 1)
            pool.memset(t2[:, NTOK:NTOK + PAD], 0.0).then_inc(pads_set, 1)
            pool.memset(lamw[:, :], 1.0).then_inc(eps_set, 1)
            pool.memset(t3[:, NTOK:TP], 0.0).then_inc(pads_set, 1)
            pool.wait_ge(cst_loaded, 16)
            for w, name in enumerate(("k1_b", "k2_b")):
                for m, mask in enumerate(("even", "odd")):
                    pool.tensor_tensor(kb[:, 2 * w + m:2 * w + m + 1], C(name), C(mask), ALU.mult).then_inc(kb_ready, 1)
            pool.wait_ge(conv_done, NSTEP)
            for b in range(2):
                pool.memset(qT[b][:, NTOK:TP], 0.0).then_inc(pads_set, 1)
            pool.memset(t4[:, NTOK:TP], 0.0).then_inc(pads_set, 1)

            def split(h):
                pool.wait_ge(part_done[0], h + 1)
                pool.tensor_tensor(stage[:, :], stage[:, :], part[0][:, :], ALU.subtract).then_inc(rest_done, 1)
                pool.wait_ge(part_done[1], h + 1)
                if h >= 1:
                    pool.wait_ge(scratch_written[h - 1], 16 * 6)
                pool.tensor_tensor(part[2][:, :], stage[:, :], part[1][:, :], ALU.subtract).then_inc(part_done[2], 1)

            split(0)
            pool.wait_ge(neglam_ready, 2)
            pool.wait_ge(eps_set, 3)
            lv = lamw[:, :].rearrange("p (r g b m) -> p r g b m", r=4, g=4, b=2)
            nl = neglam[:, H:2 * H].rearrange("p (r m) -> p r m", m=2)
            for g in range(4):
                pool.tensor_copy(lv[:, :, g, 1, :], nl).then_inc(lamw_ready, 1)
            pool.memset(prob[:, :, :, :, :], 0.0).then_inc(probs_zeroed, 1)
            pool.wait_ge(probs_zeroed, 1)
            pool.wait_ge(lamw_ready, 4)
            for u in range(16):
                n, r = u // 4, u % 4
                c = slice(16 * r, 16 * r + 16)
                pool.wait_ge(rec_done, u + 1)
                if u >= 4:
                    pool.wait_ge(scaled, u - 3)
                pool.tensor_tensor(wr[:, c], rec[:, c], lamw[:, c], ALU.mult).then_inc(wr_done, 1)
                pool.wait_ge(wr_done, u + 1)
                ev = E[:, r, :].rearrange("p (x k) -> p x k", k=NS)
                pool.tensor_tensor(ev, ev, wr[:, c].unsqueeze(2).to_broadcast([P, 16, NS]), ALU.mult).then_inc(scaled, 1)
                pool.wait_ge(scaled, u + 1)
                if n >= 2:
                    pool.wait_ge(probT_done, n - 1)
                e4 = E[:, r, :].rearrange("p (g b m k) -> p g b m k", g=4, b=2, k=NS)
                for m in range(2):
                    pool.tensor_tensor(prob[:, n % 2, :, 2 * r + m, 0:NS], e4[:, :, 0, m, :], e4[:, :, 1, m, :],
                                       ALU.add).then_inc(prob_done, 1)
            split(1)
            split(2)
            split(3)
            pool.wait_ge(trans_done[1], NPS)
            pool.memset(hidv[:, :, NTOK:TP], 0.0).then_inc(pads_set, 1)
            pool.wait_ge(htrans_done, NQ * NC)
            pool.wait_ge(lnaff_ready, 1)
            pool.tensor_tensor(t1[:, :].rearrange("p (t d) -> p t d", d=D), t6[:, :].rearrange("p (t d) -> p t d", d=D),
                               lnaff[:, D:2 * D].unsqueeze(1).to_broadcast([P, NG, D]), ALU.add).then_inc(x2b_ready, 1)

        @block.scalar
        def _(act):
            def ln_sd(L, s, eps):
                n, rows, nt, end = tiles(L, s)
                act.wait_ge(aggr_done[L], end)
                v = mv[L][0:rows, :].rearrange("p (t x) -> p t x", x=2)[:, 2 * s:2 * s + nt, 1]
                act.activation(sd[L][0:rows, 2 * s:2 * s + nt], v, ACT.Sqrt, bias=epsc[0:rows, eps:eps + 1]).then_inc(sd_done[L], 1)

            act.wait_ge(eps_set, 2)

            def z_evac(s):
                n = step_tokens(s)[0]
                act.wait_ge(trans_done[0], s + 1)
                act.activation(t1[:, s * ST:s * ST + n], PS[:, s, 0:n], ACT.Identity, bias=C("beta"), scale=C("gamma")).then_inc(z_ready, 1)

            for s in range(NSTEP):
                ln_sd(0, s, 0)
                if s == 0:
                    act.wait_ge(cst_loaded, 16)
                if s >= 2:
                    z_evac(s - 2)
            z_evac(NSTEP - 2)
            z_evac(NSTEP - 1)
            for c in range(NQ):
                act.wait_ge(dense_done, c + 1)
                act.activation(t2[:, c * QT:(c + 1) * QT], PS[:, c, 0:QT], ACT.Identity, bias=C("dense_b")).then_inc(h_ready, 1)
            def split(h):
                act.wait_ge(stage_loaded[h], 16)
                if h >= 1:
                    act.wait_ge(scratch_written[h - 1], 16 * 6)
                act.activation(part[0][:, :], stage[:, :], ACT.Copy).then_inc(part_done[0], 1)
                act.wait_ge(rest_done, h + 1)
                act.activation(part[1][:, :], stage[:, :], ACT.Copy).then_inc(part_done[1], 1)

            act.wait_ge(stage_loaded[0], 16)
            act.activation(part[0][:, :], stage[:, :], ACT.Copy).then_inc(part_done[0], 1)
            act.wait_ge(kb_ready, 4)
            for c in range(NQ):
                if c == 2:
                    act.wait_ge(rest_done, 1)
                    act.activation(part[1][:, :], stage[:, :], ACT.Copy).then_inc(part_done[1], 1)
                act.wait_ge(proj_done[0], c + 1)
                act.activation(qT[0][:, c * QT:(c + 1) * QT], PS[:, 4, 0:QT], ACT.Copy).then_inc(proj_ready[0], 1)
                act.wait_ge(proj_done[3], c + 1)
                src = PS[:, 7, 0:QT].rearrange("p (b k) -> p b k", k=NS)
                for m, mask in enumerate(("even", "odd")):
                    act.activation(kX[1][:, c * QI:(c + 1) * QI, m, :], src, ACT.Identity,
                                   bias=kb[:, 2 + m:3 + m], scale=C(mask)).then_inc(proj_ready[3], 1)
            for v in (0, 2):
                act.wait_ge(v_done, v + 1)
                act.activation(vtok[:, 4 * v:4 * v + 4, :], PS[:, 4 + v, :].rearrange("p (g c) -> p g c", g=4), ACT.Copy).then_inc(v_ready[0], 1)
            act.wait_ge(lprod_ready, 2)
            act.activation(lexp[:, :], lprod[:, :], ACT.Exp).then_inc(lexp_ready, 1)

            def o_part(n):
                act.wait_ge(pv_done, n + 1)
                if n >= 1:
                    act.wait_ge(o_ready, 4 * n)
                src = PS[:, 4:8, 0:4 * 2 * NS].rearrange("p i (g m q) -> p i g m q", g=4, m=2)[:, :, :, 0, :]
                act.activation(otmp, src, ACT.Copy, scale=C("even")).then_inc(otmp_done, 1)

            for u in range(16):
                act.wait_ge(shifted, u + 1)
                act.activation(E[:, u % 4, :], E[:, u % 4, :], ACT.Exp, scale=HD ** -0.5).then_inc(exp_done, 1)
                if u % 4 == 3 and u >= 4:
                    o_part(u // 4 - 1)
            act.wait_ge(obias_ready, 1)
            act.wait_ge(v_done, NQ)
            act.activation(t2[:, 0:NTOK], t2[:, 0:NTOK], ACT.Identity, bias=obias[:, :]).then_inc(hb_ready, 1)
            o_part(3)
            split(1)
            for hf in range(2):
                c = slice(hf * NTOK // 2, (hf + 1) * NTOK // 2)
                act.wait_ge(gcent_done, hf + 1)
                act.activation(t5[:, c], t4[:, c], ACT.Square).then_inc(gsq_done, 1)
            for hf in range(2):
                b = slice(hf * NI // 2, (hf + 1) * NI // 2)
                act.wait_ge(gvar_done, hf + 1)
                act.activation(gns[:, 2, b], PS[:, 2 * hf + 1, 0:NI // 2], ACT.Sqrt, bias=epsc[:, 1:2]).then_inc(gsd_done, 1)

            def x2_evac(s):
                act.wait_ge(trans_done[1], s + 1)
                src = PS[:, bank2[s], 0:ST].rearrange("p (b q) -> p b q", q=32)[:, :, 0:NS]
                act.activation(t3[:, s * 8 * NS:(s + 1) * 8 * NS].rearrange("p (b q) -> p b q", q=NS), src, ACT.Copy).then_inc(x2_ready, 1)
            for s in range(NPS):
                ln_sd(1, s, 1)
                if s >= 2:
                    x2_evac(s - 2)
                if s == 2:
                    split(2)
            x2_evac(NPS - 2)
            x2_evac(NPS - 1)
            for c in range(NQ):
                act.wait_ge(gfc1_done, c + 1)
                act.activation(t5[:, c * QT:(c + 1) * QT], PS[:, gbank[c], 0:QT], ACT.Relu, bias=C("gfc1_b")).then_inc(gh_ready, 1)
            split(3)

            def htok_evac(i):
                act.wait_ge(pre_done, i + 1)
                if i >= NQ:
                    act.wait_ge(htrans_done, i - NQ + 1)
                act.activation(t1[:, (i % NQ) * 512:(i % NQ + 1) * 512], PS[:, 4 + i % 2, :], ACT.Copy).then_inc(htok_ready, 1)

            def hidden_relu(i):
                c, q = i // NQ, i % NQ
                act.wait_ge(biased, i + 1)
                v = hidv[:, c, q * QT:(q + 1) * QT]
                act.activation(v, v, ACT.Relu).then_inc(hid_ready, 1)

            for cc in range(2 * NC):
                for q in range(NQ):
                    m = 8 * cc + 2 * q + 1
                    act.wait_ge(merge_done, m + 1)
                    if q == 0 and cc >= 2:
                        weights_free(act, cc)
                    evac_merged(act, m).then_inc(merged[1], 1)
                    i = NQ * (cc - 1) + q
                    if 2 <= i <= NQ * NC:
                        hidden_relu(i - 2)
                    if i == NQ * NC:
                        hidden_relu(i - 1)
                    if 0 <= i < NQ * NC:
                        htok_evac(i)

            def final_norm(s):
                act.wait_ge(shift_done, s + 1)
                for t in range(2):
                    i = 2 * s + t
                    c = slice(i * TM, (i + 1) * TM)
                    act.activation(t5[:, c], t4[:, c], ACT.Identity, bias=nms[:, i:i + 1], scale=rs[3][:, i:i + 1]).then_inc(norm_done[3], 1)

            for s in range(NPS):
                ln_sd(2, s, 1)
                if s >= 1:
                    ln_sd(3, s - 1, 1)
                if s >= 2:
                    final_norm(s - 2)
            ln_sd(3, NPS - 1, 1)
            final_norm(NPS - 2)
            final_norm(NPS - 1)

        @block.vector
        def _(dve):
            for i in range(2):
                k = slice(i * KT // 2, (i + 1) * KT // 2)
                dve.wait_ge(w_loaded[i], 16)
                v = w5.rearrange("p (k g d) -> p k d g", k=KT, g=NSH)[:, k]
                dve.tensor_reduce(weff[:, k, :], v, AX.X, ALU.add).then_inc(weff_ready, 1)

            def ln_stats(L, s, src):
                n, rows, nt, end = tiles(L, s)
                for t in range(nt):
                    i = 2 * s + t
                    dve.bn_stats(st[L][0:rows, 6 * i:6 * i + 6], src(t, rows)).then_inc(stats_done[L], 1)
                for t in range(nt):
                    i = 2 * s + t
                    dve.wait_ge(stats_done[L], i + 1)
                    dve.bn_aggr(mv[L][0:rows, 2 * i:2 * i + 2], st[L][0:rows, 6 * i:6 * i + 6]).then_inc(aggr_done[L], 1)

            def ln_norm(L, s, src, dst):
                n, rows, nt, end = tiles(L, s)
                dve.wait_ge(sd_done[L], s + 1)
                dve.reciprocal(rs[L][0:rows, 2 * s:2 * s + nt], sd[L][0:rows, 2 * s:2 * s + nt]).then_inc(rstd_done[L], 1)
                dve.wait_ge(rstd_done[L], s + 1)
                for t in range(nt):
                    i = 2 * s + t
                    dve.tensor_scalar(dst[0:rows, i * TM:(i + 1) * TM], src(t, rows), mv[L][0:rows, 2 * i:2 * i + 1],
                                      rs[L][0:rows, i:i + 1], ALU.subtract, ALU.mult).then_inc(norm_done[L], 1)

            def bank_tile(b):
                return lambda t, rows: PS[0:rows, b, t * TM:(t + 1) * TM]

            for s in range(NSTEP + 1):
                if s < NSTEP:
                    dve.wait_ge(conv_done, s + 1)
                    ln_stats(0, s, bank_tile(s))
                if s >= 1:
                    ln_norm(0, s - 1, bank_tile(s - 1), t6)
            dve.wait_ge(cst_loaded, 16)
            lam = C("lam")
            for i in range(2):
                dve.tensor_tensor(lprod[:, i * H:(i + 1) * H], lam[:, 2 * i * H:(2 * i + 1) * H],
                                  lam[:, (2 * i + 1) * H:(2 * i + 2) * H], ALU.mult).then_inc(lprod_ready, 1)
            dve.wait_ge(small_done, 1)
            dve.tensor_scalar(obias[:, :], PS[:, 7, 0:1], C("out_b"), None, ALU.add).then_inc(obias_ready, 1)
            dve.tensor_copy(lnaff[:, :], PS[:, 7, 128:128 + 2 * D]).then_inc(lnaff_ready, 1)
            dve.wait_ge(kb_ready, 4)
            for c in range(NQ):
                dve.wait_ge(proj_done[1], c + 1)
                src = PS[:, 5, 0:QT].rearrange("p (b k) -> p b k", k=NS)
                for m, mask in enumerate(("even", "odd")):
                    dve.tensor_scalar(kX[0][:, c * QI:(c + 1) * QI, m, :], src, C(mask), kb[:, m:m + 1],
                                      ALU.mult, ALU.add).then_inc(proj_ready[1], 1)
                dve.wait_ge(proj_done[2], c + 1)
                dve.tensor_copy(qT[1][:, c * QT:(c + 1) * QT], PS[:, 6, 0:QT]).then_inc(proj_ready[2], 1)
            for v in (1, 3):
                dve.wait_ge(v_done, v + 1)
                dve.tensor_copy(vtok[:, 4 * v:4 * v + 4, :], PS[:, 4 + v, :].rearrange("p (g c) -> p g c", g=4)).then_inc(v_ready[1], 1)
            dve.wait_ge(lexp_ready, 1)
            dve.tensor_tensor(neglam[:, 0:H], lexp[:, H:2 * H], lexp[:, 0:H], ALU.subtract).then_inc(neglam_ready, 1)
            dve.wait_ge(neglam_ready, 1)
            dve.tensor_scalar(neglam[:, H:2 * H], neglam[:, 0:H], -0.2, None, ALU.add).then_inc(neglam_ready, 1)

            def soft_shift(u):
                n, r = u // 4, u % 4
                c = slice(16 * r, 16 * r + 16)
                src = PS[:, r, 0:UC].rearrange("p (x k) -> p x k", k=NS)
                dve.wait_ge(scores_done, u + 1)
                dve.tensor_reduce(mx[:, c], src, AX.X, ALU.max).then_inc(max_done, 1)
                dve.wait_ge(max_done, u + 1)
                if n >= 1:
                    dve.wait_ge(prob_done, 2 * (u - 3))
                dve.tensor_tensor(E[:, r, :].rearrange("p (x k) -> p x k", k=NS), src,
                                  mx[:, c].unsqueeze(2).to_broadcast([P, 16, NS]), ALU.subtract).then_inc(shifted, 1)

            def soft_sum(u):
                r = u % 4
                c = slice(16 * r, 16 * r + 16)
                dve.wait_ge(exp_done, u + 1)
                dve.tensor_reduce(sm[:, c], E[:, r, :].rearrange("p (x k) -> p x k", k=NS), AX.X, ALU.add).then_inc(sum_done, 1)
                dve.wait_ge(sum_done, u + 1)
                if u >= 4:
                    dve.wait_ge(wr_done, u - 3)
                dve.reciprocal(rec[:, c], sm[:, c]).then_inc(rec_done, 1)

            def prob_transpose(n):
                dve.wait_ge(prob_done, 8 * (n + 1))
                if n >= 2:
                    dve.wait_ge(pv_done, n - 1)
                dve.transpose(probT[:, n % 2].rearrange("p g h q -> p (g h q)"),
                              prob[:, n % 2].rearrange("p g h k -> p (g h k)")).then_inc(probT_done, 1)

            oT = t1[:, 0:NTOK].rearrange("p (n g i q) -> p n i g q", n=NQ, g=4, i=4)

            def o_sum(n):
                dve.wait_ge(otmp_done, n + 1)
                for i in range(4):
                    src = PS[:, 4 + i, 0:4 * 2 * NS].rearrange("p (g m q) -> p g m q", g=4, m=2)[:, :, 1, :]
                    dve.scalar_tensor_tensor(out=oT[:, n, i], in0=src, scalar=C("odd"), in1=otmp[:, i],
                                             op0=ALU.mult, op1=ALU.add).then_inc(o_ready, 1)

            for u in range(16 + 2):
                if u < 16:
                    soft_shift(u)
                if 1 <= u <= 16:
                    soft_sum(u - 1)
                if u % 4 == 1 and u > 4:
                    prob_transpose(u // 4 - 1)
                    if u > 8:
                        o_sum(u // 4 - 2)
            o_sum(3)

            HT, HI = NTOK // 2, NI // 2
            dve.wait_ge(o_ready, 16)
            for hf in range(2):
                b = slice(hf * HI, (hf + 1) * HI)
                dve.tensor_reduce(gns[:, 0, b], t1[:, hf * HT:(hf + 1) * HT].rearrange("p (b k) -> p b k", k=NS),
                                  AX.X, ALU.add).then_inc(gsum_done, 1)
            for hf in range(2):
                dve.wait_ge(gmean_done, hf + 1)
                dve.tensor_tensor(t4[:, hf * HT:(hf + 1) * HT].rearrange("p (b k) -> p b k", k=NS),
                                  t1[:, hf * HT:(hf + 1) * HT].rearrange("p (b k) -> p b k", k=NS),
                                  PS[:, 2 * hf, 0:HI].unsqueeze(2).to_broadcast([P, HI, NS]), ALU.subtract).then_inc(gcent_done, 1)
            for hf in range(2):
                b = slice(hf * HI, (hf + 1) * HI)
                dve.wait_ge(gsq_done, hf + 1)
                dve.tensor_reduce(gns[:, 1, b], t5[:, hf * HT:(hf + 1) * HT].rearrange("p (b k) -> p b k", k=NS),
                                  AX.X, ALU.add).then_inc(gsqsum_done, 1)
            dve.wait_ge(gcent_done, 2)
            for hf in range(2):
                b = slice(hf * HI, (hf + 1) * HI)
                dve.wait_ge(gsd_done, hf + 1)
                dve.reciprocal(gns[:, 3, b], gns[:, 2, b]).then_inc(grstd_done, 1)
                dve.wait_ge(grstd_done, hf + 1)
                v = t4[:, hf * HT:(hf + 1) * HT].rearrange("p (b k) -> p b k", k=NS)
                dve.scalar_tensor_tensor(out=v, in0=v, scalar=C("gn_w"), in1=gns[:, 3, b].unsqueeze(2).to_broadcast([P, HI, NS]),
                                         op0=ALU.mult, op1=ALU.mult).then_inc(xn_ready, 1)

            for s in range(NPS + 1):
                if s < NPS:
                    dve.wait_ge(attn_done, s + 1)
                    ln_stats(1, s, bank_tile(bank2[s]))
                if s >= 1:
                    ln_norm(1, s - 1, bank_tile(bank2[s - 1]), t6)
            for c in range(NQ):
                dve.wait_ge(gh_ready, c + 1)
                dve.tensor_reduce(ghsum[:, c * QI:(c + 1) * QI], t5[:, c * QT:(c + 1) * QT].rearrange("p (b k) -> p b k", k=NS),
                                  AX.X, ALU.add).then_inc(ghsum_done, 1)
            dve.wait_ge(gfc2_done, 1)
            dve.tensor_scalar(gate1, PS[0:R, 5, 0:NI], 1.0 / NS, C("gate_b", R), ALU.mult, ALU.add).then_inc(gate1_done, 1)
            dve.wait_ge(gate1_done, 1)
            dve.tensor_copy(gpart[0][:, :], gate1).then_inc(gsplit, 1)
            dve.wait_ge(gsplit, 1)
            dve.tensor_tensor(grest, gate1, gpart[0][:, :], ALU.subtract).then_inc(gsplit, 1)
            dve.wait_ge(gsplit, 2)
            dve.tensor_copy(gpart[1][:, :], grest).then_inc(gsplit, 1)
            dve.wait_ge(gsplit, 3)
            dve.tensor_tensor(gpart[2][:, :], grest, gpart[1][:, :], ALU.subtract).then_inc(gsplit, 1)
            dve.tensor_scalar(gsel, gpart[0][:, :], C("gpart", R)[:, 0:1], None, ALU.mult).then_inc(gsplit, 1)
            for i in (1, 2):
                dve.wait_ge(gsplit, 4 + i)
                dve.scalar_tensor_tensor(out=gsel, in0=gpart[i][:, :], scalar=C("gpart", R)[:, i:i + 1], in1=gsel,
                                         op0=ALU.mult, op1=ALU.add).then_inc(gsplit, 1)
            dve.wait_ge(gsplit, 7)
            for j in range(NJ):
                dve.tensor_scalar(gates[:, j * NI:(j + 1) * NI], gsel, C("slice", R)[:, j:j + 1], None, ALU.mult).then_inc(gates_ready, 1)
            dve.wait_ge(b1_done, 1)
            dve.tensor_copy(b1m, PS[:, 7, 0:NC * NI].rearrange("p (c b) -> p c b", c=NC)).then_inc(b1_ready, 1)
            dve.wait_ge(b1_ready, 1)
            dve.tensor_copy(gtok, gate1.unsqueeze(2).to_broadcast([R, NI, 32])).then_inc(gtok_done, 1)

            def hidden_bias(i):
                c, q = i // NQ, i % NQ
                dve.wait_ge(htrans_done, i + 1)
                dve.tensor_tensor(hidv[:, c, q * QT:(q + 1) * QT].rearrange("p (b k) -> p b k", k=NS),
                                  PS[:, 6 + i % 2, :].rearrange("p (b k) -> p b k", k=32)[:, :, 0:NS],
                                  b1m[:, c, q * QI:(q + 1) * QI].unsqueeze(2).to_broadcast([P, QI, NS]), ALU.add).then_inc(biased, 1)

            for cc in range(2 * NC):
                for q in range(NQ):
                    m = 8 * cc + 2 * q
                    dve.wait_ge(merge_done, m + 1)
                    if q == 0 and cc >= 2:
                        weights_free(dve, cc)
                    evac_merged(dve, m).then_inc(merged[0], 1)
                    i = NQ * (cc - 1) + q
                    if 2 <= i <= NQ * NC:
                        hidden_bias(i - 2)
                    if i == NQ * NC:
                        hidden_bias(i - 1)

            for q in range(NQ):
                dve.wait_ge(ffn_done, q + 1)
                dve.tensor_tensor(t4[:, q * 512:(q + 1) * 512], PS[:, 4 + q, :], t6[:, q * 512:(q + 1) * 512], ALU.add).then_inc(res_ready, 1)

            def ln_rstd(L, s):
                dve.wait_ge(sd_done[L], s + 1)
                dve.reciprocal(rs[L][:, 2 * s:2 * s + 2], sd[L][:, 2 * s:2 * s + 2]).then_inc(rstd_done[L], 1)
                dve.wait_ge(rstd_done[L], s + 1)

            def affine(s):
                for t in range(2):
                    i = 2 * s + t
                    v = t4[:, i * TM:(i + 1) * TM]
                    dve.scalar_tensor_tensor(out=v, in0=v, scalar=mv[2][:, 2 * i:2 * i + 1], in1=lnaff[:, 0:D],
                                             op0=ALU.subtract, op1=ALU.mult).then_inc(aff_part, 1)
                ln_rstd(2, s)
                if s == 0:
                    dve.wait_ge(x2b_ready, 1)
                for t in range(2):
                    i = 2 * s + t
                    v = t4[:, i * TM:(i + 1) * TM]
                    dve.wait_ge(aff_part, i + 1)
                    dve.scalar_tensor_tensor(out=v, in0=v, scalar=rs[2][:, i:i + 1], in1=t1[:, i * TM:(i + 1) * TM],
                                             op0=ALU.mult, op1=ALU.add).then_inc(aff_done, 1)

            def final_shift(s):
                ln_rstd(3, s)
                m = mv[3][:, :].rearrange("p (t x) -> p t x", x=2)[:, 2 * s:2 * s + 2, 0]
                dve.scalar_tensor_tensor(out=nms[:, 2 * s:2 * s + 2], in0=m, scalar=-1.0, in1=rs[3][:, 2 * s:2 * s + 2],
                                         op0=ALU.mult, op1=ALU.mult).then_inc(shift_done, 1)

            def t4_tile(s):
                return lambda t, rows: t4[0:rows, s * ST + t * TM:s * ST + (t + 1) * TM]

            for s in range(NPS + 2):
                if s < NPS:
                    dve.wait_ge(res_ready, s // 2 + 1)
                    ln_stats(2, s, t4_tile(s))
                if 1 <= s <= NPS:
                    affine(s - 1)
                    dve.wait_ge(aff_done, 2 * s)
                    ln_stats(3, s - 1, t4_tile(s - 1))
                if s >= 2:
                    final_shift(s - 2)

        @block.tensor
        def _(pe):
            def transposes(L, s, bank, src):
                n, rows, nt, end = tiles(L, s)
                pe.wait_ge(norm_done[L], end)
                for t in range(nt):
                    i = 2 * s + t
                    mm = pe.transpose(PS[:, bank, t * TM:t * TM + rows], src[0:rows, i * TM:(i + 1) * TM], ident[0:rows, 0:rows])
                mm.then_inc(trans_done[L], 1)

            def conv(s):
                n, rows, nt = step_tokens(s)
                pe.wait_ge(x_loaded[s], 16)
                for t in range(nt):
                    for k in range(KT):
                        if s == 0 and t == 0 and k % (KT // 2) == 0:
                            pe.wait_ge(weff_ready, k // (KT // 2) + 1)
                        mm = pe.matmul(PS[0:rows, s, t * TM:(t + 1) * TM], xs(s)[:, k, t * TM:t * TM + rows], weff[:, k, :],
                                       start=(k == 0), stop=(k == KT - 1))
                mm.then_inc(conv_done, 1)

            for s in range(NSTEP):
                conv(s)
                if s == 1:
                    pe.wait_ge(cst_loaded, 16)
                if s >= 2:
                    transposes(0, s - 2, s - 2, t6)
            transposes(0, NSTEP - 2, NSTEP - 2, t6)
            transposes(0, NSTEP - 1, NSTEP - 1, t6)
            pe.matmul(PS[:, 7, 0:1], C("o"), C("gn_b"), start=True, stop=True)
            pe.matmul(PS[:, 7, 128:256], C("coef", NE + 1), C("ln_g", NE + 1), start=True, stop=True)
            pe.matmul(PS[:, 7, 256:384], C("coef", NE + 1), C("ln_b", NE + 1), start=True, stop=True).then_inc(small_done, 1)
            for c in range(NQ):
                pe.wait_ge(z_ready, steps_for[c])
                pe.matmul(PS[:, c, 0:QT], C("dense_w"), t1[:, c * QT:(c + 1) * QT], start=True, stop=True).then_inc(dense_done, 1)
            pe.wait_ge(z_ready, NSTEP)
            pe.wait_ge(obias_ready, 1)
            pe.wait_ge(lnaff_ready, 1)
            for c in range(NQ):
                pe.wait_ge(h_ready, c + 1)
                for w, name in enumerate(("q1", "k1", "q2", "k2")):
                    if c >= 1:
                        pe.wait_ge(proj_ready[w], (2 if w in (1, 3) else 1) * c)
                    pe.matmul(PS[:, 4 + w, 0:QT], C(name), t2[:, c * QT:(c + 1) * QT], start=True, stop=True).then_inc(proj_done[w], 1)
            pe.wait_ge(pads_set, 1)
            for v in range(4):
                pe.wait_ge(proj_ready[v], 2 * NQ if v in (1, 3) else NQ)
                for g in range(4):
                    for i in range(4):
                        c = ((4 * v + g) * 4 + i) * NS
                        mm = pe.matmul(PS[32 * i:32 * i + 32, 4 + v, g * D:(g + 1) * D], t2[:, c:c + 32], C("v"), start=True, stop=True)
                mm.then_inc(v_done, 1)

            def scores(u):
                n, r = u // 4, u % 4
                if n >= 1:
                    pe.wait_ge(shifted, u - 3)
                for g in range(4):
                    for b in range(2):
                        for i in range(4):
                            im = (n * 4 + g) * 4 + i
                            c = (g * 2 + b) * 2 * NS
                            mm = pe.matmul(PS[32 * i:32 * i + 32, r, c:c + 2 * NS],
                                           qT[b][32 * r:32 * r + 32, im * NS:im * NS + 32],
                                           kX[b][32 * r:32 * r + 32, im, :, :], start=True, stop=True)
                mm.then_inc(scores_done, 1)

            def values(n):
                pe.wait_ge(probT_done, n + 1)
                if n >= 1:
                    pe.wait_ge(o_ready, 4 * n)
                for i in range(4):
                    for g in range(4):
                        for r in range(4):
                            mm = pe.matmul(PS[32 * r:32 * r + 32, 4 + i, g * 2 * NS:(g + 1) * 2 * NS],
                                           vtok[32 * i:32 * i + 32, 4 * n + g, 32 * r:32 * r + 32],
                                           probT[32 * i:32 * i + 32, n % 2, g, 2 * r:2 * r + 2, 0:NS], start=True, stop=True)
                mm.then_inc(pv_done, 1)

            pe.wait_ge(pads_set, 5)
            pe.wait_ge(v_ready[0], 2)
            pe.wait_ge(v_ready[1], 2)
            for n in range(NQ):
                for r in range(4):
                    scores(4 * n + r)
                if n >= 1:
                    values(n - 1)
            values(NQ - 1)
            HI = NI // 2
            for hf in range(2):
                pe.wait_ge(gsum_done, hf + 1)
                pe.matmul(PS[:, 2 * hf, 0:HI], C("gnsum"), gns[:, 0, hf * HI:(hf + 1) * HI], start=True, stop=True).then_inc(gmean_done, 1)
            for hf in range(2):
                pe.wait_ge(gsqsum_done, hf + 1)
                pe.matmul(PS[:, 2 * hf + 1, 0:HI], C("gnsum"), gns[:, 1, hf * HI:(hf + 1) * HI], start=True, stop=True).then_inc(gvar_done, 1)
            pe.wait_ge(hb_ready, 1)
            for s in range(NPS):
                if s == 3:
                    pe.wait_ge(xn_ready, 2)
                elif s == 0:
                    pe.wait_ge(xn_ready, 1)
                for g in range(2):
                    for i in range(4):
                        c = ((2 * s + g) * 4 + i) * NS
                        o = PS[32 * i:32 * i + 32, bank2[s], g * D:(g + 1) * D]
                        pe.matmul(o, t4[:, c:c + 32], C("o"), start=True, stop=False)
                        mm = pe.matmul(o, t2[:, c:c + 32], ident, start=False, stop=True)
                mm.then_inc(attn_done, 1)
                if s >= 2:
                    transposes(1, s - 2, bank2[s - 2], t6)
            transposes(1, NPS - 2, bank2[NPS - 2], t6)
            transposes(1, NPS - 1, bank2[NPS - 1], t6)
            for c in range(NQ):
                pe.wait_ge(x2_ready, 2 * c + 2)
                pe.matmul(PS[:, gbank[c], 0:QT], C("gfc1"), t3[:, c * QT:(c + 1) * QT], start=True, stop=True).then_inc(gfc1_done, 1)
            pe.wait_ge(ghsum_done, NQ)
            pe.matmul(PS[0:R, 5, 0:NI], C("gfc2"), ghsum, start=True, stop=True).then_inc(gfc2_done, 1)
            pe.wait_ge(gate1_done, 1)
            for c in range(NC):
                mm = pe.matmul(PS[:, 7, c * NI:(c + 1) * NI], C("tvb1", R)[:, c * P:(c + 1) * P], gate1, start=True, stop=True)
            mm.then_inc(b1_done, 1)
            pe.wait_ge(gates_ready, NJ)

            def merge(cc, q):
                w = wrow[:, (cc % 2) * SJ * P:(cc % 2 + 1) * SJ * P].rearrange("p (s m) -> p s m", m=P)
                if q == 0:
                    pe.wait_ge(wrow_loaded[cc % 2], 16 * (len(TERMS) + 1) * (cc // 2 + 1))
                for m in range(8 * cc + 2 * q, 8 * cc + 2 * q + 2):
                    if m >= 2:
                        pe.wait_ge(merged[m % 2], m // 2)
                    for i in range(8):
                        mm = pe.matmul(PS[:, 2 * (m % 2) + i // 4, (i % 4) * P:(i % 4 + 1) * P], w[:, 8 * (m % 8) + i, :], gates[:, :],
                                       start=True, stop=True)
                    mm.then_inc(merge_done, 1)

            def hidden_transpose(i):
                pe.wait_ge(htok_ready, i + 1)
                if i >= 2:
                    pe.wait_ge(biased, i - 1)
                for g in range(4):
                    c = (i % NQ) * 512 + g * P
                    mm = pe.transpose(PS[:, 6 + i % 2, g * P:(g + 1) * P], t1[:, c:c + P], ident)
                mm.then_inc(htrans_done, 1)

            def apply1(c, q):
                i = NQ * c + q
                if i >= 2:
                    pe.wait_ge(htok_ready, i - 1)
                for b in range(QI):
                    im = q * QI + b
                    mm = pe.matmul(PS[32 * (b % 4):32 * (b % 4) + 32, 4 + i % 2, (b // 4) * P:(b // 4 + 1) * P],
                                   t3[:, im * NS:im * NS + 32], wm[c % 2][:, im, :], start=True, stop=True)
                mm.then_inc(pre_done, 1)
                if i >= 1:
                    hidden_transpose(i - 1)
                if i == NQ * NC - 1:
                    hidden_transpose(i)

            def apply2(c, q):
                if c == 0 and q == 0:
                    pe.wait_ge(hid_ready, NQ * NC)
                    pe.wait_ge(pads_set, 6)
                    pe.wait_ge(gtok_done, 1)
                if c == 0:
                    for g in range(4):
                        im = q * QI + 4 * g
                        pe.matmul(PS[:, 4 + q, g * D:(g + 1) * D], gtok[:, im:im + 4, :].rearrange("p b q -> p (b q)"),
                                  C("tvb2", R), start=(g == 0), stop=False, skip_group_check=True)
                for b in range(QI):
                    im = q * QI + b
                    mm = pe.matmul(PS[32 * (b % 4):32 * (b % 4) + 32, 4 + q, (b // 4) * D:(b // 4 + 1) * D],
                                   hidv[:, c, im * NS:im * NS + 32], wm[c % 2][:, im, :],
                                   start=False, stop=(c == NC - 1), skip_group_check=True)
                if c == NC - 1:
                    mm.then_inc(ffn_done, 1)
                elif q == NQ - 1:
                    mm.then_inc(applied, 1)

            for cc in range(2 * NC + 1):
                if cc >= 1:
                    pe.wait_ge(merged[0], 4 * cc)
                    pe.wait_ge(merged[1], 4 * cc)
                for q in range(NQ):
                    if cc < 2 * NC:
                        merge(cc, q)
                    if 1 <= cc <= NC:
                        apply1(cc - 1, q)
                    elif cc > NC:
                        apply2(cc - 1 - NC, q)


def _layout(np, i):
    f4 = np.float32
    a = {k: np.asarray(v) for k, v in i.items()}
    x = a["x"]
    xp = np.zeros((NI, x.shape[1] + 1, x.shape[2] + 1, 3), f4)
    xp[:, 1:, 1:] = x
    win = np.zeros((NI, 5, 5, 18, 18, 3), f4)
    for r in range(5):
        for c in range(5):
            win[:, r, c] = xp[:, 16 * r:16 * r + 18, 16 * c:16 * c + 18]
    k = 18 * 18 * 3
    xcol = np.zeros((KT * P, NTOK), f4)
    xcol[:k] = win.reshape(NTOK, k).T
    xcol[k] = 1.0
    xcol = xcol.reshape(KT, P, NTOK).transpose(1, 0, 2)
    parts = []
    for s in range(NSTEP):
        n = step_tokens(s)[0]
        parts.append(xcol[:, :, s * ST:s * ST + n].reshape(P, KT * n))
    w = a["L0_tok_conv_w"].reshape(16, 16, NSH, 3, D)
    w5 = np.zeros((18, 18, 3, NSH, D), f4)
    for g, (r, c) in enumerate(((1, 1), (1, 0), (1, 2), (0, 1), (2, 1))):
        w5[r:r + 16, c:c + 16, :, g] = w[:, :, g]
    wc = np.zeros((KT * P, NSH, D), f4)
    wc[:k] = w5.reshape(k, NSH, D)
    wc[k, 0] = a["L0_tok_conv_b"]
    wc = wc.reshape(KT, P, NSH * D).transpose(1, 0, 2).reshape(P, KT * NSH * D)

    cst = np.zeros((P, NCONST), f4)

    def put(name, v):
        lo, hi = COL[name]
        v = v.reshape(v.shape[0], -1)
        assert v.shape[1] == hi - lo, name
        cst[0:v.shape[0], lo:hi] = v
    put("dense_w", a["L0_tok_dense_w"])
    for name, src in (("q1", "Q1"), ("k1", "K1"), ("q2", "Q2"), ("k2", "K2"), ("v", "V"), ("o", "out")):
        put(name, a[f"L0_attn_{src}_w"].T)
    put("gfc1", a["L0_ffn_gfc1_w"].T)
    def rows(tv, base, first_only):
        v = np.zeros((R, base.size), f4)
        for t in range(len(TERMS)):
            for e in range(NE):
                for j in range(NJ):
                    if not first_only or (t, j) == (0, 0):
                        v[t * RE + e * NJ + j] = tv[e]
        for k in range(3 * NJ):
            if not first_only or k == 0:
                v[RB + k] = base
        return v
    put("gfc2", rows(a["L0_ffn_gfc2_w"], np.zeros(D, f4), False).T)
    gpart = np.zeros((R, 3), f4)
    for t, (_, gp) in enumerate(TERMS):
        gpart[t * RE:(t + 1) * RE, gp] = 1
    gpart[RB:, 0] = 1
    put("gpart", gpart)
    for name, src in (("gamma", "tok_gamma"), ("beta", "tok_beta"), ("dense_b", "tok_dense_b"), ("k1_b", "attn_K1_b"),
                      ("k2_b", "attn_K2_b"), ("gn_w", "attn_gn_w"), ("gn_b", "attn_gn_b"), ("out_b", "attn_out_b"),
                      ("gfc1_b", "ffn_gfc1_b")):
        put(name, a["L0_" + src].reshape(P, 1))
    put("gate_b", rows(a["L0_ffn_gfc2_b"], np.ones(1, f4), False))
    p = np.arange(P)
    put("even", (p // HD % 2 == 0).astype(f4).reshape(P, 1))
    put("odd", (p // HD % 2 == 1).astype(f4).reshape(P, 1))
    put("slice", np.tile(np.eye(NJ, dtype=f4), (R // NJ, 1)))
    put("tvb1", rows(a["L0_ffn_tv_b1"], a["L0_ffn_b1"], True))
    put("tvb2", rows(a["L0_ffn_tv_b2"], a["L0_ffn_b2"], True))
    put("ln_g", np.concatenate([a["L0_ffn_ln_g"][None], a["L0_ffn_tv_ln_g"]]))
    put("ln_b", np.concatenate([a["L0_ffn_ln_b"][None], a["L0_ffn_tv_ln_b"]]))
    coef = np.full((NE + 1, P), 0.03, f4)
    coef[0] = 1 - 0.03 * NE
    put("coef", coef)
    put("gnsum", (p[:, None] // 32 == p[None] // 32).astype(f4) / (32 * NS))
    put("ident", np.eye(P, dtype=f4))
    lam = np.concatenate([a["L0_attn_lambda_" + n].reshape(-1) for n in ("q1", "k1", "q2", "k2")])
    put("lam", np.broadcast_to(lam, (P, 4 * H)))

    def halves(tv, base):
        tv = tv.reshape(P, 2, HE)
        base = base.reshape(P, 2, HB)
        return [np.concatenate([tv[:, h], base[:, h]], 1) for h in range(2)]

    def w1(v):
        return v.reshape(-1, NC, NJ, SJ, D).transpose(0, 2, 1, 3, 4)

    def w2(v):
        return v.reshape(-1, NJ, SJ, NC, P).transpose(0, 1, 3, 2, 4)
    stages = halves(w1(a["L0_ffn_tv_W1"]), w1(a["L0_ffn_W1"])) + halves(w2(a["L0_ffn_tv_W2"]), w2(a["L0_ffn_W2"]))
    return {
        "consts": cst, "conv_filter": np.ascontiguousarray(wc), "windows": np.concatenate(parts, 1),
        "ffn_weights": np.stack(stages),
    }


def kernel(**inputs):
    import numpy as _np
    import concourse.bacc as _bacc
    from concourse import mybir as _mybir
    from concourse.bass_utils import run_bass_kernel_spmd as _run

    arrays = _layout(_np, inputs)
    nc = _bacc.Bacc("TRN2", target_bir_lowering=False, num_devices=1)
    f32 = _mybir.dt.float32
    d = {n: nc.dram_tensor(n, v.shape, f32, kind="ExternalInput").ap() for n, v in arrays.items()}
    out = nc.dram_tensor("out", (NTOK, D), f32, kind="ExternalOutput").ap()
    cols = [KT * ST * s for s in range(NSTEP)] + [KT * NTOK]
    xcol = [d["windows"][:, cols[s]:cols[s + 1]].rearrange("p (k n) -> p k n", k=KT) for s in range(NSTEP)]
    bf16 = _mybir.dt.bfloat16
    sce = nc.dram_tensor("parts_tv", (2, 3, P, 2 * HE), bf16, kind="Internal").ap()
    scb = nc.dram_tensor("parts_base", (2, 3, P, 2 * HB), bf16, kind="Internal").ap()
    build(nc, d["consts"], d["conv_filter"], xcol, d["ffn_weights"], sce, scb, out)
    r = _run(nc, [arrays], core_ids=[0])
    return r.results[0]["out"].reshape(NI, NS, D)
```

```python
import concourse.bass as bass
from concourse import mybir
from contextlib import ExitStack

P = 128
NI, NS = 64, 25
NTOK = NI * NS
D, H, HD = 128, 8, 16
F, NE = 512, 8
KT = 8
NP = KT // 2
NSH = 5
TM = 128
ST = 2 * TM
NSTEP = -(-NTOK // ST)
NTILE = -(-NTOK // TM)
NQ = 4
QI, QT = NI // NQ, NTOK // NQ
NG = NI // 4
NC = F // P
PAD = 8
TP = NTOK + PAD
NPS = NG // 2
LAG = 3
NUNIT = NG // 2
UI = NI // NUNIT
UC = 2 * 2 * H * NS
UX = 2 * 2 * H
ES = 3

NJ = 2
SJ = P // NJ
TERMS = [(0, 0), (0, 1), (0, 2), (1, 0), (1, 1), (2, 0)]
RE = NE * NJ
RB = len(TERMS) * RE
R = RB + 3 * NJ
WROW = NC * SJ * P
NU = P // RE
HE, HB = WROW // NU // 2, NJ * WROW // P // 2
HS = HE + HB

_COLS = [("gamma", 1), ("beta", 1), ("ident", 128), ("dense_w", 128), ("dense_b", 1),
         ("q1", 128), ("k1", 128), ("q2", 128), ("k2", 128), ("v", 128), ("o", 128),
         ("gfc1", 128), ("gfc2", R), ("gpart", 3), ("k1_b", 1), ("k2_b", 1),
         ("gn_w", 1), ("gn_b", 1), ("out_b", 1), ("gfc1_b", 1), ("gate_b", 1), ("even", 1), ("odd", 1),
         ("slice", NJ), ("tvb1", F), ("tvb2", D), ("ln_g", D), ("ln_b", D), ("coef", 128),
         ("gnsum", 128), ("lam", 4 * H)]
COL, _at = {}, 0
for _n, _w in _COLS:
    COL[_n] = (_at, _at + _w)
    _at += _w
NCONST = _at
NFIRST = COL["q1"][0]


def step_tokens(s):
    n = min(ST, NTOK - s * ST)
    return n, min(n, TM), -(-n // TM)


def build(nc, cst_d, wconv_d, xcol_d, tvw_d, sce_d, scb_d, out_d):
    f32 = mybir.dt.float32
    bf16 = mybir.dt.bfloat16
    ALU = mybir.AluOpType
    ACT = mybir.ActivationFunctionType
    AX = mybir.AxisListType
    ctx = ExitStack()
    with ctx:
        def sb(name, cols, rows=P, dt=f32):
            return ctx.enter_context(nc.sbuf_tensor(name, [rows, cols], dt))

        def sem(name):
            return ctx.enter_context(nc.semaphore(name))

        cst = sb("cst", NCONST)
        arena = sb("arena", 2 * NI * P)
        hid = sb("hid", NC * TP)
        wrow = sb("wrow", 2 * SJ * P, R, bf16)
        stage = sb("stage", HS)
        part = [sb(f"part{i}", HS, P, bf16) for i in range(3)]
        t1 = sb("t1", NG * P)
        t2 = sb("t2", TP)
        t3 = sb("t3", TP)
        t4 = sb("t4", NG * P)
        t5 = sb("t5", NG * P)
        t6 = sb("t6", NG * P)
        PS = ctx.enter_context(nc.psum_tensor("PS", [P, 8, 512], f32))

        def C(name, rows=P):
            a, b = COL[name]
            return cst[0:rows, a:b]

        def xs(s):
            n = step_tokens(s)[0]
            return arena[:, KT * ST * s:KT * ST * s + KT * n].rearrange("p (k n) -> p k n", k=KT)

        w5 = hid[:, 0:KT * NSH * D]
        weff = hid[:, KT * NSH * D:KT * (NSH + 1) * D].rearrange("p (k d) -> p k d", k=KT)
        at = [0]

        def take(n):
            at[0] += n
            assert at[0] <= 2 * NI * P
            return arena[:, at[0] - n:at[0]]
        qT = [take(NTOK + PAD) for _ in range(2)]
        kX = take(2 * 2 * NTOK).rearrange("p (u b m k) -> p u b m k", u=NUNIT, b=2, m=2)
        vtok = take(NG * D).rearrange("p (g c) -> p g c", g=NG)
        E = take(ES * UC).rearrange("p (u c) -> p u c", u=ES)
        prob = take(2 * 4 * H * 32).rearrange("p (n g h k) -> p n g h k", n=2, g=4, h=H)
        kE = hid[:, 0:2 * 2 * H * UI * NS].rearrange("p (s b h i k) -> p s b h i k", s=2, b=2, h=H, i=UI)
        kEd = hid[:, 0:2 * 2 * H * UI * NS].rearrange("p (s b r c) -> p s b r c", s=2, b=2, r=4)
        probT = t6[:, 0:2 * 4 * H * 32].rearrange("p (n g h q) -> p n g h q", n=2, g=4, h=H)
        otmp = t5[:, NTOK:NTOK + QT].rearrange("p (i g q) -> p i g q", i=4, g=4)
        gns = t3[:, 0:4 * NI].rearrange("p (a b) -> p a b", a=4)
        wm = [arena[:, i * NI * P:(i + 1) * NI * P].rearrange("p (b m) -> p b m", b=NI) for i in range(2)]
        hidv = hid[:, :].rearrange("p (c n) -> p c n", c=NC)
        b1m = t4[:, 0:NC * NI].rearrange("p (c b) -> p c b", c=NC)
        gate1 = t4[0:R, 256:256 + NI]
        grest = t4[0:R, 320:320 + NI]
        gsel = t4[0:R, 384:384 + NI]
        ghsum = t4[:, 448:448 + NI]
        gtok = t5[0:R, 0:NI * 32].rearrange("p (b q) -> p b q", b=NI)
        gpart = [sb(f"gpart{i}", NI, R, bf16) for i in range(3)]
        gates = sb("gates", NJ * NI, R, bf16)

        mx = sb("mx", ES * UX)
        sm = sb("sm", ES * UX)
        rec = sb("rec", ES * UX)
        wr = sb("wr", ES * UX)
        lamw = sb("lamw", UX)
        lprod = sb("lprod", 2 * H)
        lexp = sb("lexp", 2 * H)
        neglam = sb("neglam", 2 * H)
        kb = sb("kb", 4)
        epsc = sb("epsc", 2)
        obias = sb("obias", 1)
        lnaff = sb("lnaff", 2 * D)
        mvl = sb("mvl", 8 * (NPS + LAG))
        sdl = sb("sdl", 4 * (NPS + LAG))
        rsl = sb("rsl", 4 * (NPS + LAG))
        nms = sb("nms", 4 * (NPS + LAG))
        st = [sb(f"st{i}", NG * 6) for i in range(4)]
        mv = [sb(f"mv{i}", NG * 2) for i in range(2)]
        sd = [sb(f"sd{i}", NG) for i in range(2)]
        rs = [sb(f"rs{i}", NG) for i in range(2)]

        w_loaded = [sem(f"w_loaded{i}") for i in range(KT // 2)]
        x_loaded = [[sem(f"x_loaded{i}_{j}") for i in range(NSTEP)] for j in range(NP)]
        first_loaded = sem("first_loaded")
        cst_loaded = sem("cst_loaded")
        stage_loaded = [sem(f"stage_loaded{i}") for i in range(4)]
        part_done = [sem(f"part_done{i}") for i in range(3)]
        rest_done = sem("rest_done")
        scratch_written = [sem(f"scratch_written{i}") for i in range(4)]
        wrow_loaded = [sem(f"wrow_loaded{i}") for i in range(2)]
        stored = sem("stored")
        weff_ready = sem("weff_ready")
        conv_done = sem("conv_done")
        eps_set = sem("eps_set")
        root_warm = sem("root_warm")
        stats_done = [sem(f"stats_done{i}") for i in range(4)]
        aggr_done = [sem(f"aggr_done{i}") for i in range(4)]
        sd_done = [sem(f"sd_done{i}") for i in range(2)]
        rstd_done = [sem(f"rstd_done{i}") for i in range(2)]
        norm_done = [sem(f"norm_done{i}") for i in range(4)]
        trans_done = [sem(f"trans_done{i}") for i in range(3)]
        z_ready = sem("z_ready")
        dense_done = sem("dense_done")
        h_ready = sem("h_ready")
        small_done = sem("small_done")
        obias_ready = sem("obias_ready")
        lnaff_ready = sem("lnaff_ready")
        kb_ready = sem("kb_ready")
        pads_set = sem("pads_set")
        probs_zeroed = sem("probs_zeroed")
        spread_zeroed = sem("spread_zeroed")
        keys_spread = [sem(f"keys_spread{i}") for i in range(2)]
        proj_done = [sem(f"proj_done{w}") for w in range(4)]
        proj_ready = [sem(f"proj_ready{w}") for w in range(4)]
        v_done = sem("v_done")
        v_ready = [sem("v_ready_act"), sem("v_ready_dve")]
        lprod_ready = sem("lprod_ready")
        lexp_ready = sem("lexp_ready")
        neglam_ready = sem("neglam_ready")
        lamw_ready = sem("lamw_ready")
        hb_ready = sem("hb_ready")
        scores_done = sem("scores_done")
        max_done = sem("max_done")
        shifted = sem("shifted")
        exp_done = sem("exp_done")
        sum_done = sem("sum_done")
        rec_done = sem("rec_done")
        wr_done = sem("wr_done")
        scaled = sem("scaled")
        prob_done = sem("prob_done")
        probT_done = sem("probT_done")
        pv_done = sem("pv_done")
        otmp_done = sem("otmp_done")
        o_ready = sem("o_ready")
        gsum_done = sem("gsum_done")
        gmean_done = sem("gmean_done")
        gcent_done = sem("gcent_done")
        gsq_done = sem("gsq_done")
        gsqsum_done = sem("gsqsum_done")
        gvar_done = sem("gvar_done")
        gsd_done = sem("gsd_done")
        grstd_done = sem("grstd_done")
        xn_ready = sem("xn_ready")
        attn_done = sem("attn_done")
        x2_ready = sem("x2_ready")
        gfc1_done = sem("gfc1_done")
        gh_ready = sem("gh_ready")
        ghsum_done = sem("ghsum_done")
        gfc2_done = sem("gfc2_done")
        gate1_done = sem("gate1_done")
        gsplit = sem("gsplit")
        gtok_done = sem("gtok_done")
        gates_ready = sem("gates_ready")
        b1_done = sem("b1_done")
        b1_ready = sem("b1_ready")
        merge_done = sem("merge_done")
        merged = [sem("merged_by_dve"), sem("merged_by_act")]
        applied = sem("applied")
        pre_done = sem("pre_done")
        htok_ready = sem("htok_ready")
        htrans_done = sem("htrans_done")
        biased = sem("biased")
        hid_ready = sem("hid_ready")
        ffn_done = sem("ffn_done")
        res_ready = sem("res_ready")
        x2b_ready = sem("x2b_ready")
        shift_done = sem("shift_done")
        last_sd_done = sem("last_sd_done")
        last_rstd_done = sem("last_rstd_done")
        aff_part = sem("aff_part")
        aff_done = sem("aff_done")

        ident = C("ident")
        steps_for = [-(-min(NTOK, QT * (c + 1)) // ST) for c in range(NQ)]
        bank2 = [0, 1, 2, 4, 5, 6, 7, 3]
        gbank = [bank2[2 * c] for c in range(NQ)]
        HT, HI = NTOK // 2, NI // 2
        gmean = [PS[:, 3, 2 * i * HI:(2 * i + 1) * HI] for i in range(2)]
        gvar = [PS[:, 3, (2 * i + 1) * HI:(2 * i + 2) * HI] for i in range(2)]

        def tiles(L, s):
            if L == 0:
                n, rows, nt = step_tokens(s)
                return n, rows, nt, min(2 * s + nt, NTILE)
            return ST, P, 2, 2 * s + 2

        def slot(j):
            return slice(4 * j + (2 if j >= NPS else 0), 4 * j + (4 if j >= LAG else 2))

        def last_tile(L, i):
            return 2 * (i - i % 2) + i % 2 + (4 * LAG + 2 if L == 3 else 0)

        def merge_bank(m):
            return 2 * (m % 4) if m < 8 else 2 * (m % 2)

        def merged_views(m):
            cc, k = m // 8, m % 8
            b0 = merge_bank(m)
            src = PS[:, b0:b0 + 2, :].rearrange("p n (s j b) -> p (n s) j b", j=NJ, b=NI)
            dst = wm[cc % 2].rearrange("p b (j s) -> p s j b", j=NJ)[:, 8 * k:8 * k + 8]
            return src, dst

        def weights_free(eng, cc):
            if cc - 2 < NC:
                eng.wait_ge(pre_done, NQ * (cc - 1))
            else:
                eng.wait_ge(applied, cc - 1 - NC)

        def evac_merged(eng, m):
            src, dst = merged_views(m)
            if m % 2:
                return eng.activation(dst, src, ACT.Copy)
            return eng.tensor_copy(dst, src)

        block = ctx.enter_context(nc.Block())

        @block.sync
        def _(sp):
            def load_filter(i):
                c = slice(2 * i * NSH * D, 2 * (i + 1) * NSH * D)
                sp.dma_start(w5[:, c], wconv_d[:, c]).then_inc(w_loaded[i], 16)

            def load_windows(s, j):
                k = slice(2 * j, 2 * j + 2)
                sp.dma_start(xs(s)[:, k], xcol_d[s][:, k]).then_inc(x_loaded[j][s], 16)

            for j in range(NP):
                load_filter(j)
                if j == NP - 1:
                    sp.dma_start(cst[:, 0:NFIRST], cst_d[:, 0:NFIRST]).then_inc(first_loaded, 16)
                for s in range(NSTEP):
                    load_windows(s, j)
            sp.dma_start(cst[:, NFIRST:], cst_d[:, NFIRST:]).then_inc(cst_loaded, 16)
            def store_parts(h, which=range(3)):
                m, hv = h // 2, h % 2
                for i in which:
                    sp.wait_ge(part_done[i], h + 1)
                    sp.dma_start(sce_d[m, i][:, hv * HE:(hv + 1) * HE], part[i][:, 0:HE]).then_inc(scratch_written[h], 16)
                    sp.dma_start(scb_d[m, i][:, hv * HB:(hv + 1) * HB], part[i][:, HE:HS]).then_inc(scratch_written[h], 16)

            def load_stage(h):
                if h >= 1:
                    sp.wait_ge(part_done[2], h)
                sp.dma_start(stage[:, :], tvw_d[h]).then_inc(stage_loaded[h], 16)

            def load_rows(cc):
                m, c, slot = cc // NC, cc % NC, cc % 2
                if cc >= 2:
                    sp.wait_ge(merge_done, 8 * (cc - 1))
                row = 0
                for i in range(3):
                    copies = sum(t[0] == i for t in TERMS)
                    src = sce_d[m, i].rearrange("(r u) n -> r (u n)", u=NU)[:, c * SJ * P:(c + 1) * SJ * P]
                    for _ in range(copies):
                        sp.dma_start(wrow[row:row + RE, slot * SJ * P:(slot + 1) * SJ * P], src).then_inc(wrow_loaded[slot], 16)
                        row += RE
                src = scb_d[m].rearrange("i (j u) n -> (i j) (u n)", j=NJ)[:, c * SJ * P:(c + 1) * SJ * P]
                sp.dma_start(wrow[RB:R, slot * SJ * P:(slot + 1) * SJ * P], src).then_inc(wrow_loaded[slot], 16)

            def spread_keys(u):
                if u % 2 == 0:
                    sp.wait_ge(proj_ready[1], 2 * (u // 2 + 1))
                    sp.wait_ge(proj_ready[3], 2 * (u // 2 + 1))
                if u < 2:
                    sp.wait_ge(spread_zeroed, u + 1)
                else:
                    sp.wait_ge(scores_done, u - 1)
                for r in range(4):
                    f = slice(32 * r, 32 * r + 32)
                    sp.dma_start(kEd[f, u % 2, :, r, :], kX[f, u].rearrange("p b m k -> p b (m k)")).then_inc(keys_spread[u % 2], 16)

            load_stage(0)
            spread_keys(0)
            spread_keys(1)
            store_parts(0, (0,))
            spread_keys(2)
            spread_keys(3)
            store_parts(0, (1,))
            spread_keys(4)
            spread_keys(5)
            store_parts(0, (2,))
            for u in range(6, NUNIT):
                spread_keys(u)
            load_stage(1)
            store_parts(1)
            load_stage(2)
            for h in range(2):
                sp.wait_ge(scratch_written[h], 16 * 6)
            load_rows(0)
            load_rows(1)
            store_parts(2)
            load_stage(3)
            load_rows(2)
            load_rows(3)
            store_parts(3)
            for h in range(2, 4):
                sp.wait_ge(scratch_written[h], 16 * 6)
            for cc in range(4, 2 * NC):
                load_rows(cc)
            out_v = out_d.rearrange("(g i q) d -> i q g d", i=4, q=NS)
            for s in range(0, NPS, 2):
                sp.wait_ge(norm_done[3], 2 * (s + 2))
                for i in range(4):
                    src = t5[32 * i:32 * i + NS, s * ST:(s + 2) * ST].rearrange("p (g d) -> p g d", d=D)
                    sp.dma_start(out_v[i][:, 2 * s:2 * s + 4, :], src).then_inc(stored, 16)
            sp.wait_ge(stored, 16 * 4 * (NPS // 2))

        @block.gpsimd
        def _(pool):
            pool.memset(epsc[:, 0:1], 1e-3).then_inc(eps_set, 1)
            pool.memset(epsc[:, 1:2], 1e-5).then_inc(eps_set, 1)
            pool.memset(t2[:, NTOK:NTOK + PAD], 0.0).then_inc(pads_set, 1)
            pool.memset(lamw[:, :], 1.0).then_inc(eps_set, 1)
            pool.memset(t3[:, NTOK:TP], 0.0).then_inc(pads_set, 1)
            pool.wait_ge(cst_loaded, 16)
            for w, name in enumerate(("k1_b", "k2_b")):
                for m, mask in enumerate(("even", "odd")):
                    pool.tensor_tensor(kb[:, 2 * w + m:2 * w + m + 1], C(name), C(mask), ALU.mult).then_inc(kb_ready, 1)
            pool.wait_ge(conv_done, NSTEP)
            for b in range(2):
                pool.memset(qT[b][:, NTOK:TP], 0.0).then_inc(pads_set, 1)
            pool.memset(t4[:, NTOK:TP], 0.0).then_inc(pads_set, 1)

            for i in range(2):
                pool.memset(kEd[:, i], 0.0).then_inc(spread_zeroed, 1)

            def split(h):
                pool.wait_ge(part_done[0], h + 1)
                pool.tensor_tensor(stage[:, :], stage[:, :], part[0][:, :], ALU.subtract).then_inc(rest_done, 1)
                pool.wait_ge(part_done[1], h + 1)
                if h >= 1:
                    pool.wait_ge(scratch_written[h - 1], 16 * 6)
                pool.tensor_tensor(part[2][:, :], stage[:, :], part[1][:, :], ALU.subtract).then_inc(part_done[2], 1)

            split(0)
            pool.wait_ge(neglam_ready, 2)
            pool.wait_ge(eps_set, 3)
            lv = lamw[:, :].rearrange("p (g b h) -> p g b h", g=2, b=2)
            for g in range(2):
                pool.tensor_copy(lv[:, g, 1, :], neglam[:, H:2 * H]).then_inc(lamw_ready, 1)
            pool.memset(prob[:, :, :, :, :], 0.0).then_inc(probs_zeroed, 1)
            pool.wait_ge(probs_zeroed, 1)
            pool.wait_ge(lamw_ready, 2)
            for u in range(NUNIT):
                n, g, slot = u // 2, 2 * (u % 2), u % ES
                c = slice(UX * slot, UX * slot + UX)
                pool.wait_ge(rec_done, u + 1)
                if u >= ES:
                    pool.wait_ge(scaled, u - ES + 1)
                pool.tensor_tensor(wr[:, c], rec[:, c], lamw[:, :], ALU.mult).then_inc(wr_done, 1)
                pool.wait_ge(wr_done, u + 1)
                ev = E[:, slot, :].rearrange("p (x k) -> p x k", k=NS)
                pool.tensor_tensor(ev, ev, wr[:, c].unsqueeze(2).to_broadcast([P, UX, NS]), ALU.mult).then_inc(scaled, 1)
                pool.wait_ge(scaled, u + 1)
                if n >= 2:
                    pool.wait_ge(probT_done, n - 1)
                e4 = E[:, slot, :].rearrange("p (g b h k) -> p g b h k", g=2, b=2, k=NS)
                pool.tensor_tensor(prob[:, n % 2, g:g + 2, :, 0:NS], e4[:, :, 0], e4[:, :, 1],
                                   ALU.add).then_inc(prob_done, 1)
            split(1)
            split(2)
            split(3)
            pool.wait_ge(trans_done[1], NPS)
            pool.memset(hidv[:, :, NTOK:TP], 0.0).then_inc(pads_set, 1)
            pool.wait_ge(htrans_done, NQ * NC)
            pool.wait_ge(lnaff_ready, 1)
            pool.tensor_tensor(t1[:, :].rearrange("p (t d) -> p t d", d=D), t6[:, :].rearrange("p (t d) -> p t d", d=D),
                               lnaff[:, D:2 * D].unsqueeze(1).to_broadcast([P, NG, D]), ALU.add).then_inc(x2b_ready, 1)
            pool.wait_ge(x2b_ready, 1)
            for s in range(NPS):
                pool.wait_ge(norm_done[2], 2 * (s + 1))
                c = slice(s * ST, (s + 1) * ST)
                v = t4[:, c].rearrange("p (t d) -> p t d", d=D)
                pool.tensor_tensor(v, v, lnaff[:, 0:D].unsqueeze(1).to_broadcast([P, 2, D]), ALU.mult).then_inc(aff_part, 1)
                pool.wait_ge(aff_part, s + 1)
                pool.tensor_tensor(t4[:, c], t4[:, c], t1[:, c], ALU.add).then_inc(aff_done, 1)

        @block.scalar
        def _(act):
            def ln_sd(L, s, eps):
                n, rows, nt, end = tiles(L, s)
                act.wait_ge(aggr_done[L], end)
                if L == 1 and s == 0:
                    act.wait_ge(root_warm, 1)
                v = mv[L][0:rows, :].rearrange("p (t x) -> p t x", x=2)[:, 2 * s:2 * s + nt, 1]
                act.activation(sd[L][0:rows, 2 * s:2 * s + nt], v, ACT.Sqrt, bias=epsc[0:rows, eps:eps + 1]).then_inc(sd_done[L], 1)

            act.wait_ge(eps_set, 2)
            act.activation(sd[1][:, 0:2], epsc[:, :], ACT.Sqrt).then_inc(root_warm, 1)

            def z_evac(s):
                n = step_tokens(s)[0]
                act.wait_ge(trans_done[0], s + 1)
                act.activation(t1[:, s * ST:s * ST + n], PS[:, s, 0:n], ACT.Identity, bias=C("beta"), scale=C("gamma")).then_inc(z_ready, 1)

            for s in range(NSTEP):
                ln_sd(0, s, 0)
                if s == 0:
                    act.wait_ge(first_loaded, 16)
                if s >= 2:
                    z_evac(s - 2)
            def h_evac(c):
                act.wait_ge(dense_done, c + 1)
                act.activation(t2[:, c * QT:(c + 1) * QT], PS[:, c, 0:QT], ACT.Identity, bias=C("dense_b")).then_inc(h_ready, 1)

            h_evac(0)
            z_evac(NSTEP - 2)
            h_evac(1)
            z_evac(NSTEP - 1)
            h_evac(2)
            h_evac(3)

            def split_first(h):
                act.wait_ge(stage_loaded[h], 16)
                if h >= 1:
                    act.wait_ge(scratch_written[h - 1], 16 * 6)
                act.activation(part[0][:, :], stage[:, :], ACT.Copy).then_inc(part_done[0], 1)

            def split_second(h):
                act.wait_ge(rest_done, h + 1)
                act.activation(part[1][:, :], stage[:, :], ACT.Copy).then_inc(part_done[1], 1)

            split_first(0)
            act.wait_ge(kb_ready, 4)
            for c in range(NQ):
                act.wait_ge(proj_done[0], c + 1)
                act.activation(qT[0][:, c * QT:(c + 1) * QT], PS[:, 4, 0:QT], ACT.Copy).then_inc(proj_ready[0], 1)
                act.wait_ge(proj_done[3], c + 1)
                src = PS[:, 7, 0:QT].rearrange("p (u k) -> p u k", u=2)
                for m, mask in enumerate(("even", "odd")):
                    act.activation(kX[:, 2 * c:2 * c + 2, 1, m, :], src, ACT.Identity,
                                   bias=kb[:, 2 + m:3 + m], scale=C(mask)).then_inc(proj_ready[3], 1)
            act.wait_ge(lprod_ready, 2)
            act.activation(lexp[:, :], lprod[:, :], ACT.Exp).then_inc(lexp_ready, 1)

            def v_evac(v):
                act.wait_ge(v_done, v + 1)
                act.activation(vtok[:, 4 * v:4 * v + 4, :], PS[:, 4 + v, :].rearrange("p (g c) -> p g c", g=4), ACT.Copy).then_inc(v_ready[0], 1)

            def o_part(k):
                h = k % 2
                act.wait_ge(pv_done, k + 1)
                if k >= 2:
                    act.wait_ge(o_ready, 2 * (k - 1))
                src = PS[:, 4 + 2 * h:6 + 2 * h, 0:4 * 2 * NS].rearrange("p i (g m q) -> p i g m q", g=4, m=2)[:, :, :, 0, :]
                act.activation(otmp[:, 2 * h:2 * h + 2], src, ACT.Copy, scale=C("even")).then_inc(otmp_done, 1)

            def group_square(hf):
                c = slice(hf * HT, (hf + 1) * HT)
                act.wait_ge(gcent_done, hf + 1)
                act.activation(t5[:, c], t4[:, c], ACT.Square).then_inc(gsq_done, 1)

            def group_sd(hf):
                act.wait_ge(gvar_done, hf + 1)
                act.activation(gns[:, 2, hf * HI:(hf + 1) * HI], gvar[hf], ACT.Sqrt, bias=epsc[:, 1:2]).then_inc(gsd_done, 1)

            for u in range(NUNIT):
                act.wait_ge(shifted, u + 1)
                act.activation(E[:, u % ES, :], E[:, u % ES, :], ACT.Exp, scale=HD ** -0.5).then_inc(exp_done, 1)
                if u == 0:
                    split_second(0)
                if u < 2:
                    v_evac(2 * u)
                if u == 2:
                    act.wait_ge(obias_ready, 1)
                    act.wait_ge(v_done, NQ)
                    act.activation(t2[:, 0:NTOK], t2[:, 0:NTOK], ACT.Identity, bias=obias[:, :]).then_inc(hb_ready, 1)
                if u >= 5:
                    o_part(u - 5)
            split_first(1)
            o_part(3)
            group_square(0)
            o_part(4)
            o_part(5)
            group_sd(0)
            o_part(6)
            split_second(1)
            o_part(7)
            group_square(1)
            ln_sd(1, 0, 1)
            ln_sd(1, 1, 1)
            group_sd(1)
            ln_sd(1, 2, 1)

            def x2_evac(s):
                act.wait_ge(trans_done[1], s + 1)
                src = PS[:, bank2[s], 0:ST].rearrange("p (b q) -> p b q", q=32)[:, :, 0:NS]
                act.activation(t3[:, s * 8 * NS:(s + 1) * 8 * NS].rearrange("p (b q) -> p b q", q=NS), src, ACT.Copy).then_inc(x2_ready, 1)
            def gate_relu(c):
                act.wait_ge(gfc1_done, c + 1)
                act.activation(t5[:, c * QT:(c + 1) * QT], PS[:, gbank[c], 0:QT], ACT.Relu, bias=C("gfc1_b")).then_inc(gh_ready, 1)

            for s in range(NPS):
                if s >= 3:
                    ln_sd(1, s, 1)
                if s >= 2:
                    x2_evac(s - 2)
                if s == 4:
                    split_first(2)
            gate_relu(0)
            x2_evac(NPS - 2)
            gate_relu(1)
            x2_evac(NPS - 1)
            gate_relu(2)
            gate_relu(3)
            split_second(2)

            def htok_evac(i):
                act.wait_ge(pre_done, i + 1)
                if i >= NQ:
                    act.wait_ge(htrans_done, i - NQ + 1)
                act.activation(t1[:, (i % NQ) * 512:(i % NQ + 1) * 512], PS[:, 4 + i % 2, :], ACT.Copy).then_inc(htok_ready, 1)

            def hidden_relu(i):
                c, q = i // NQ, i % NQ
                act.wait_ge(biased, i + 1)
                v = hidv[:, c, q * QT:(q + 1) * QT]
                act.activation(v, v, ACT.Relu).then_inc(hid_ready, 1)

            for cc in range(2 * NC):
                for q in range(NQ):
                    m = 8 * cc + 2 * q + 1
                    act.wait_ge(merge_done, m + 1)
                    if q == 0 and cc >= 2:
                        weights_free(act, cc)
                    evac_merged(act, m).then_inc(merged[1], 1)
                    i = NQ * (cc - 1) + q
                    if 2 <= i <= NQ * NC:
                        hidden_relu(i - 2)
                    if i == NQ * NC:
                        hidden_relu(i - 1)
                    if 0 <= i < NQ * NC:
                        htok_evac(i)
                    if (cc, q) == (1, 0):
                        split_first(3)
                    if (cc, q) == (1, 3):
                        split_second(3)

            def last_sd(j):
                if j < NPS:
                    act.wait_ge(aggr_done[2], 2 * (j + 1))
                if j >= LAG:
                    act.wait_ge(aggr_done[3], 2 * (j - LAG + 1))
                v = mvl[:, :].rearrange("p (t x) -> p t x", x=2)[:, slot(j), 1]
                act.activation(sdl[:, slot(j)], v, ACT.Sqrt, bias=epsc[:, 1:2]).then_inc(last_sd_done, 1)

            def last_norm(L, s, dst):
                act.wait_ge(shift_done, s + 1 if L == 2 else s + LAG + 1)
                for t in range(2):
                    i = 2 * s + t
                    c, k = slice(i * TM, (i + 1) * TM), last_tile(L, i)
                    act.activation(dst[:, c], t4[:, c], ACT.Identity, bias=nms[:, k:k + 1], scale=rsl[:, k:k + 1]).then_inc(norm_done[L], 1)

            for j in range(NPS + LAG):
                last_sd(j)
                if j > LAG:
                    last_norm(3, j - 1 - LAG, t5)
                if j < NPS:
                    last_norm(2, j, t4)
            last_norm(3, NPS - 1, t5)

        @block.vector
        def _(dve):
            for i in range(KT // 2):
                k = slice(2 * i, 2 * i + 2)
                dve.wait_ge(w_loaded[i], 16)
                v = w5.rearrange("p (k g d) -> p k d g", k=KT, g=NSH)[:, k]
                dve.tensor_reduce(weff[:, k, :], v, AX.X, ALU.add).then_inc(weff_ready, 1)

            def ln_stats(L, s, src):
                n, rows, nt, end = tiles(L, s)
                for t in range(nt):
                    i = 2 * s + t
                    dve.bn_stats(st[L][0:rows, 6 * i:6 * i + 6], src(t, rows)).then_inc(stats_done[L], 1)
                for t in range(nt):
                    i = 2 * s + t
                    dve.wait_ge(stats_done[L], i + 1)
                    dve.bn_aggr(mv[L][0:rows, 2 * i:2 * i + 2], st[L][0:rows, 6 * i:6 * i + 6]).then_inc(aggr_done[L], 1)

            def ln_norm(L, s, src, dst):
                n, rows, nt, end = tiles(L, s)
                dve.wait_ge(sd_done[L], s + 1)
                dve.reciprocal(rs[L][0:rows, 2 * s:2 * s + nt], sd[L][0:rows, 2 * s:2 * s + nt]).then_inc(rstd_done[L], 1)
                dve.wait_ge(rstd_done[L], s + 1)
                for t in range(nt):
                    i = 2 * s + t
                    dve.tensor_scalar(dst[0:rows, i * TM:(i + 1) * TM], src(t, rows), mv[L][0:rows, 2 * i:2 * i + 1],
                                      rs[L][0:rows, i:i + 1], ALU.subtract, ALU.mult).then_inc(norm_done[L], 1)

            def bank_tile(b):
                return lambda t, rows: PS[0:rows, b, t * TM:(t + 1) * TM]

            for s in range(NSTEP + 1):
                if s < NSTEP:
                    dve.wait_ge(conv_done, s + 1)
                    ln_stats(0, s, bank_tile(s))
                if s >= 1:
                    ln_norm(0, s - 1, bank_tile(s - 1), t6)
            dve.wait_ge(cst_loaded, 16)
            lam = C("lam")
            for i in range(2):
                dve.tensor_tensor(lprod[:, i * H:(i + 1) * H], lam[:, 2 * i * H:(2 * i + 1) * H],
                                  lam[:, (2 * i + 1) * H:(2 * i + 2) * H], ALU.mult).then_inc(lprod_ready, 1)
            dve.wait_ge(small_done, 1)
            dve.tensor_scalar(obias[:, :], PS[:, 7, 0:1], C("out_b"), None, ALU.add).then_inc(obias_ready, 1)
            dve.tensor_copy(lnaff[:, :], PS[:, 7, 128:128 + 2 * D]).then_inc(lnaff_ready, 1)
            dve.wait_ge(kb_ready, 4)
            for c in range(NQ):
                dve.wait_ge(proj_done[1], c + 1)
                src = PS[:, 5, 0:QT].rearrange("p (u k) -> p u k", u=2)
                for m, mask in enumerate(("even", "odd")):
                    dve.tensor_scalar(kX[:, 2 * c:2 * c + 2, 0, m, :], src, C(mask), kb[:, m:m + 1],
                                      ALU.mult, ALU.add).then_inc(proj_ready[1], 1)
                dve.wait_ge(proj_done[2], c + 1)
                dve.tensor_copy(qT[1][:, c * QT:(c + 1) * QT], PS[:, 6, 0:QT]).then_inc(proj_ready[2], 1)

            def v_evac(v):
                dve.wait_ge(v_done, v + 1)
                dve.tensor_copy(vtok[:, 4 * v:4 * v + 4, :], PS[:, 4 + v, :].rearrange("p (g c) -> p g c", g=4)).then_inc(v_ready[1], 1)

            def soft_shift(u):
                bank, slot = 2 * (u % 2), u % ES
                c = slice(UX * slot, UX * slot + UX)
                src = PS[:, bank:bank + 2, 0:UC // 2].rearrange("p g (x k) -> p g x k", k=NS)
                mxv = mx[:, c].rearrange("p (g x) -> p g x", g=2)
                dve.wait_ge(scores_done, u + 1)
                dve.tensor_reduce(mxv, src, AX.X, ALU.max).then_inc(max_done, 1)
                dve.wait_ge(max_done, u + 1)
                if u >= ES:
                    dve.wait_ge(prob_done, u - ES + 1)
                dve.tensor_tensor(E[:, slot, :].rearrange("p (g x k) -> p g x k", g=2, k=NS), src,
                                  mxv.unsqueeze(3).to_broadcast([P, 2, UX // 2, NS]), ALU.subtract).then_inc(shifted, 1)

            def soft_sum(u):
                slot = u % ES
                c = slice(UX * slot, UX * slot + UX)
                dve.wait_ge(exp_done, u + 1)
                dve.tensor_reduce(sm[:, c], E[:, slot, :].rearrange("p (x k) -> p x k", k=NS), AX.X, ALU.add).then_inc(sum_done, 1)
                dve.wait_ge(sum_done, u + 1)
                if u >= ES:
                    dve.wait_ge(wr_done, u - ES + 1)
                dve.reciprocal(rec[:, c], sm[:, c]).then_inc(rec_done, 1)

            def prob_transpose(n):
                dve.wait_ge(prob_done, 2 * (n + 1))
                if n >= 2:
                    dve.wait_ge(pv_done, 2 * (n - 1))
                dve.transpose(probT[:, n % 2].rearrange("p g h q -> p (g h q)"),
                              prob[:, n % 2].rearrange("p g h k -> p (g h k)")).then_inc(probT_done, 1)

            oT = t1[:, 0:NTOK].rearrange("p (n g i q) -> p n i g q", n=NQ, g=4, i=4)

            def o_sum(k):
                n, h = k // 2, k % 2
                dve.wait_ge(otmp_done, k + 1)
                for i in (2 * h, 2 * h + 1):
                    src = PS[:, 4 + i, 0:4 * 2 * NS].rearrange("p (g m q) -> p g m q", g=4, m=2)[:, :, 1, :]
                    dve.scalar_tensor_tensor(out=oT[:, n, i], in0=src, scalar=C("odd"), in1=otmp[:, i],
                                             op0=ALU.mult, op1=ALU.add).then_inc(o_ready, 1)

            def by_image(t, hf):
                return t[:, hf * HT:(hf + 1) * HT].rearrange("p (b k) -> p b k", k=NS)

            def group_sum(hf):
                dve.wait_ge(o_ready, 8 * (hf + 1))
                dve.tensor_reduce(gns[:, 0, hf * HI:(hf + 1) * HI], by_image(t1, hf), AX.X, ALU.add).then_inc(gsum_done, 1)

            def group_centre(hf):
                dve.wait_ge(gmean_done, hf + 1)
                dve.tensor_tensor(by_image(t4, hf), by_image(t1, hf), gmean[hf].unsqueeze(2).to_broadcast([P, HI, NS]),
                                  ALU.subtract).then_inc(gcent_done, 1)

            def group_square_sum(hf):
                dve.wait_ge(gsq_done, hf + 1)
                dve.tensor_reduce(gns[:, 1, hf * HI:(hf + 1) * HI], by_image(t5, hf), AX.X, ALU.add).then_inc(gsqsum_done, 1)

            def group_scale(hf):
                b = slice(hf * HI, (hf + 1) * HI)
                dve.wait_ge(gsd_done, hf + 1)
                dve.reciprocal(gns[:, 3, b], gns[:, 2, b]).then_inc(grstd_done, 1)
                dve.wait_ge(grstd_done, hf + 1)
                v = by_image(t4, hf)
                dve.wait_ge(gcent_done, hf + 1)
                dve.scalar_tensor_tensor(out=v, in0=v, scalar=C("gn_w"), in1=gns[:, 3, b].unsqueeze(2).to_broadcast([P, HI, NS]),
                                         op0=ALU.mult, op1=ALU.mult).then_inc(xn_ready, 1)

            soft_shift(0)
            dve.wait_ge(lexp_ready, 1)
            dve.tensor_tensor(neglam[:, 0:H], lexp[:, H:2 * H], lexp[:, 0:H], ALU.subtract).then_inc(neglam_ready, 1)
            dve.wait_ge(neglam_ready, 1)
            dve.tensor_scalar(neglam[:, H:2 * H], neglam[:, 0:H], -0.2, None, ALU.add).then_inc(neglam_ready, 1)
            soft_shift(1)
            soft_sum(0)
            v_evac(1)
            v_evac(3)
            for u in range(2, NUNIT):
                soft_shift(u)
                soft_sum(u - 1)
                if u in (3, 5, 7):
                    prob_transpose((u - 3) // 2)
                if u >= 5:
                    o_sum(u - 5)
            soft_sum(NUNIT - 1)
            o_sum(3)
            group_sum(0)
            group_centre(0)
            prob_transpose(3)
            o_sum(4)
            o_sum(5)
            group_square_sum(0)
            group_scale(0)
            o_sum(6)
            o_sum(7)
            group_sum(1)

            def attn_stats(s):
                dve.wait_ge(attn_done, s + 1)
                ln_stats(1, s, bank_tile(bank2[s]))

            attn_stats(0)
            group_centre(1)
            attn_stats(1)
            group_square_sum(1)
            attn_stats(2)
            group_scale(1)

            for s in range(NPS + 1):
                if 3 <= s < NPS:
                    attn_stats(s)
                if s >= 1:
                    ln_norm(1, s - 1, bank_tile(bank2[s - 1]), t6)
            for c in range(NQ):
                dve.wait_ge(gh_ready, c + 1)
                dve.tensor_reduce(ghsum[:, c * QI:(c + 1) * QI], t5[:, c * QT:(c + 1) * QT].rearrange("p (b k) -> p b k", k=NS),
                                  AX.X, ALU.add).then_inc(ghsum_done, 1)
            dve.wait_ge(gfc2_done, 1)
            dve.tensor_scalar(gate1, PS[0:R, 1, 0:NI], 1.0 / NS, C("gate_b", R), ALU.mult, ALU.add).then_inc(gate1_done, 1)
            dve.wait_ge(gate1_done, 1)
            dve.tensor_copy(gpart[0][:, :], gate1).then_inc(gsplit, 1)

            def select(i):
                dve.scalar_tensor_tensor(out=gsel, in0=gpart[i][:, :], scalar=C("gpart", R)[:, i:i + 1], in1=gsel,
                                         op0=ALU.mult, op1=ALU.add).then_inc(gsplit, 1)

            dve.wait_ge(gsplit, 1)
            dve.tensor_tensor(grest, gate1, gpart[0][:, :], ALU.subtract).then_inc(gsplit, 1)
            dve.tensor_scalar(gsel, gpart[0][:, :], C("gpart", R)[:, 0:1], None, ALU.mult).then_inc(gsplit, 1)
            dve.wait_ge(gsplit, 2)
            dve.tensor_copy(gpart[1][:, :], grest).then_inc(gsplit, 1)
            dve.wait_ge(gsplit, 4)
            dve.tensor_tensor(gpart[2][:, :], grest, gpart[1][:, :], ALU.subtract).then_inc(gsplit, 1)
            select(1)
            dve.wait_ge(gsplit, 6)
            select(2)
            dve.wait_ge(gsplit, 7)
            for j in range(NJ):
                dve.tensor_scalar(gates[:, j * NI:(j + 1) * NI], gsel, C("slice", R)[:, j:j + 1], None, ALU.mult).then_inc(gates_ready, 1)

            def hidden_bias(i):
                c, q = i // NQ, i % NQ
                dve.wait_ge(htrans_done, i + 1)
                dve.tensor_tensor(hidv[:, c, q * QT:(q + 1) * QT].rearrange("p (b k) -> p b k", k=NS),
                                  PS[:, 6 + i % 2, :].rearrange("p (b k) -> p b k", k=32)[:, :, 0:NS],
                                  b1m[:, c, q * QI:(q + 1) * QI].unsqueeze(2).to_broadcast([P, QI, NS]), ALU.add).then_inc(biased, 1)

            for cc in range(2 * NC):
                for q in range(NQ):
                    m = 8 * cc + 2 * q
                    dve.wait_ge(merge_done, m + 1)
                    if q == 0 and cc >= 2:
                        weights_free(dve, cc)
                    evac_merged(dve, m).then_inc(merged[0], 1)
                    i = NQ * (cc - 1) + q
                    if i == 0:
                        dve.wait_ge(b1_done, 1)
                        dve.tensor_copy(b1m, PS[:, 6, 0:NC * NI].rearrange("p (c b) -> p c b", c=NC)).then_inc(b1_ready, 1)
                    if i == 1:
                        dve.wait_ge(b1_ready, 1)
                        dve.tensor_copy(gtok, gate1.unsqueeze(2).to_broadcast([R, NI, 32])).then_inc(gtok_done, 1)
                    if 2 <= i <= NQ * NC:
                        hidden_bias(i - 2)
                    if i == NQ * NC:
                        hidden_bias(i - 1)

            def residual(q):
                dve.wait_ge(ffn_done, q + 1)
                dve.tensor_tensor(t4[:, q * 512:(q + 1) * 512], PS[:, 4 + q, :], t6[:, q * 512:(q + 1) * 512], ALU.add).then_inc(res_ready, 1)

            def last_stats(L, s):
                for i in (2 * s, 2 * s + 1):
                    dve.bn_stats(st[L][:, 6 * i:6 * i + 6], t4[:, i * TM:(i + 1) * TM]).then_inc(stats_done[L], 1)
                for i in (2 * s, 2 * s + 1):
                    k = last_tile(L, i)
                    dve.wait_ge(stats_done[L], i + 1)
                    dve.bn_aggr(mvl[:, 2 * k:2 * k + 2], st[L][:, 6 * i:6 * i + 6]).then_inc(aggr_done[L], 1)

            def last_shift(j):
                dve.wait_ge(last_sd_done, j + 1)
                dve.reciprocal(rsl[:, slot(j)], sdl[:, slot(j)]).then_inc(last_rstd_done, 1)
                dve.wait_ge(last_rstd_done, j + 1)
                m = mvl[:, :].rearrange("p (t x) -> p t x", x=2)[:, slot(j), 0]
                dve.scalar_tensor_tensor(out=nms[:, slot(j)], in0=m, scalar=-1.0, in1=rsl[:, slot(j)],
                                         op0=ALU.mult, op1=ALU.mult).then_inc(shift_done, 1)

            for j in range(NPS + LAG + 1):
                if j % 2 == 0 and j < NPS:
                    residual(j // 2)
                if j < NPS:
                    dve.wait_ge(res_ready, j // 2 + 1)
                    last_stats(2, j)
                if j >= 1:
                    last_shift(j - 1)
                if LAG <= j < NPS + LAG:
                    dve.wait_ge(aff_done, j - LAG + 1)
                    last_stats(3, j - LAG)

        @block.tensor
        def _(pe):
            def transposes(L, s, bank, src):
                n, rows, nt, end = tiles(L, s)
                pe.wait_ge(norm_done[L], end)
                for t in range(nt):
                    i = 2 * s + t
                    mm = pe.transpose(PS[:, bank, t * TM:t * TM + rows], src[0:rows, i * TM:(i + 1) * TM], ident[0:rows, 0:rows])
                mm.then_inc(trans_done[L], 1)

            def conv(s, j):
                n, rows, nt = step_tokens(s)
                pe.wait_ge(x_loaded[j][s], 16)
                for t in range(nt):
                    for k in range(2 * j, 2 * j + 2):
                        if s == 0 and t == 0 and k == 2 * j:
                            pe.wait_ge(weff_ready, j + 1)
                        mm = pe.matmul(PS[0:rows, s, t * TM:(t + 1) * TM], xs(s)[:, k, t * TM:t * TM + rows], weff[:, k, :],
                                       start=(t == 0 and k == 0), stop=(k == KT - 1), skip_group_check=True)
                if j == NP - 1:
                    mm.then_inc(conv_done, 1)

            def dense(c):
                pe.wait_ge(z_ready, steps_for[c])
                pe.matmul(PS[:, c, 0:QT], C("dense_w"), t1[:, c * QT:(c + 1) * QT], start=True, stop=True).then_inc(dense_done, 1)

            for j in range(NP - 1):
                for s in range(NSTEP):
                    conv(s, j)
            for s in range(NSTEP):
                conv(s, NP - 1)
                if s == 1:
                    pe.wait_ge(first_loaded, 16)
                if s >= 2:
                    transposes(0, s - 2, s - 2, t6)
                if s == NSTEP - 2:
                    dense(0)
            dense(1)
            transposes(0, NSTEP - 2, NSTEP - 2, t6)
            dense(2)
            transposes(0, NSTEP - 1, NSTEP - 1, t6)
            pe.wait_ge(cst_loaded, 16)
            pe.matmul(PS[:, 7, 0:1], C("o"), C("gn_b"), start=True, stop=True)
            pe.matmul(PS[:, 7, 128:256], C("coef", NE + 1), C("ln_g", NE + 1), start=True, stop=True)
            pe.matmul(PS[:, 7, 256:384], C("coef", NE + 1), C("ln_b", NE + 1), start=True, stop=True).then_inc(small_done, 1)
            dense(3)
            pe.wait_ge(obias_ready, 1)
            pe.wait_ge(lnaff_ready, 1)
            for c in range(NQ):
                pe.wait_ge(h_ready, c + 1)
                for w, name in enumerate(("q1", "k1", "q2", "k2")):
                    if c >= 1:
                        pe.wait_ge(proj_ready[w], (2 if w in (1, 3) else 1) * c)
                    pe.matmul(PS[:, 4 + w, 0:QT], C(name), t2[:, c * QT:(c + 1) * QT], start=True, stop=True).then_inc(proj_done[w], 1)

            def v_proj():
                for v in range(4):
                    pe.wait_ge(proj_ready[v], 2 * NQ if v in (1, 3) else NQ)
                    for g in range(4):
                        for i in range(4):
                            c = ((4 * v + g) * 4 + i) * NS
                            mm = pe.matmul(PS[32 * i:32 * i + 32, 4 + v, g * D:(g + 1) * D], t2[:, c:c + 32], C("v"), start=True, stop=True)
                    mm.then_inc(v_done, 1)

            def scores(u):
                slot = u % 2
                pe.wait_ge(keys_spread[slot], 16 * 4 * (u // 2 + 1))
                if u >= 2:
                    pe.wait_ge(shifted, u - 1)
                for g in range(2):
                    for b in range(2):
                        for i in range(4):
                            im = u * UI + g * 4 + i
                            mm = pe.matmul(PS[32 * i:32 * i + 32, 2 * slot + g, b * H * NS:(b + 1) * H * NS],
                                           qT[b][:, im * NS:im * NS + 32], kE[:, slot, b, :, g * 4 + i, :], start=True, stop=True)
                mm.then_inc(scores_done, 1)

            def values(k):
                n, h = k // 2, k % 2
                pe.wait_ge(probT_done, n + 1)
                if k >= 2:
                    pe.wait_ge(o_ready, 2 * (k - 1))
                for i in (2 * h, 2 * h + 1):
                    for g in range(4):
                        for r in range(4):
                            mm = pe.matmul(PS[32 * r:32 * r + 32, 4 + i, g * 2 * NS:(g + 1) * 2 * NS],
                                           vtok[32 * i:32 * i + 32, 4 * n + g, 32 * r:32 * r + 32],
                                           probT[32 * i:32 * i + 32, n % 2, g, 2 * r:2 * r + 2, 0:NS], start=True, stop=True)
                mm.then_inc(pv_done, 1)

            pe.wait_ge(pads_set, 5)
            scores(0)
            scores(1)
            v_proj()
            for u in range(2, 6):
                scores(u)
            pe.wait_ge(v_ready[0], 2)
            pe.wait_ge(v_ready[1], 2)
            values(0)
            scores(6)
            values(1)
            scores(7)
            values(2)
            values(3)

            def group_mean(hf):
                pe.wait_ge(gsum_done, hf + 1)
                if hf == 0:
                    pe.wait_ge(shifted, NUNIT)
                else:
                    pe.wait_ge(gsd_done, hf)
                pe.matmul(gmean[hf], C("gnsum"), gns[:, 0, hf * HI:(hf + 1) * HI], start=True, stop=True).then_inc(gmean_done, 1)

            def group_var(hf):
                pe.wait_ge(gsqsum_done, hf + 1)
                pe.matmul(gvar[hf], C("gnsum"), gns[:, 1, hf * HI:(hf + 1) * HI], start=True, stop=True).then_inc(gvar_done, 1)

            def out_rows(s):
                for g in range(2):
                    for i in range(4):
                        yield g, ((2 * s + g) * 4 + i) * NS, PS[32 * i:32 * i + 32, bank2[s], g * D:(g + 1) * D]

            def residual(s):
                for g, c, o in out_rows(s):
                    pe.matmul(o, t2[:, c:c + 32], ident, start=(g == 0), stop=False, skip_group_check=True)

            def out_proj(s):
                for g, c, o in out_rows(s):
                    mm = pe.matmul(o, t4[:, c:c + 32], C("o"), start=False, stop=True, skip_group_check=True)
                mm.then_inc(attn_done, 1)

            def gate_hidden(c):
                pe.wait_ge(x2_ready, 2 * c + 2)
                pe.matmul(PS[:, gbank[c], 0:QT], C("gfc1"), t3[:, c * QT:(c + 1) * QT], start=True, stop=True).then_inc(gfc1_done, 1)

            pe.wait_ge(hb_ready, 1)
            pe.wait_ge(shifted, NUNIT - 1)
            residual(0)
            residual(1)
            values(4)
            group_mean(0)
            values(5)
            residual(2)
            values(6)
            group_var(0)
            values(7)
            pe.wait_ge(xn_ready, 1)
            out_proj(0)
            pe.wait_ge(o_ready, 14)
            residual(3)
            group_mean(1)
            out_proj(1)
            out_proj(2)
            residual(4)
            group_var(1)
            pe.wait_ge(o_ready, 16)
            residual(5)
            residual(6)
            pe.wait_ge(xn_ready, 2)
            for s in range(3, NPS):
                if s == NPS - 1:
                    residual(s)
                out_proj(s)
                transposes(1, s - 3, bank2[s - 3], t6)
                if s == 6:
                    gate_hidden(0)
            transposes(1, NPS - 3, bank2[NPS - 3], t6)
            gate_hidden(1)
            transposes(1, NPS - 2, bank2[NPS - 2], t6)
            gate_hidden(2)
            transposes(1, NPS - 1, bank2[NPS - 1], t6)
            gate_hidden(3)
            pe.wait_ge(ghsum_done, NQ)
            pe.matmul(PS[0:R, 1, 0:NI], C("gfc2"), ghsum, start=True, stop=True).then_inc(gfc2_done, 1)
            pe.wait_ge(gates_ready, NJ)

            def merge(cc, q):
                w = wrow[:, (cc % 2) * SJ * P:(cc % 2 + 1) * SJ * P].rearrange("p (s m) -> p s m", m=P)
                if q == 0:
                    pe.wait_ge(wrow_loaded[cc % 2], 16 * (len(TERMS) + 1) * (cc // 2 + 1))
                for m in range(8 * cc + 2 * q, 8 * cc + 2 * q + 2):
                    if m >= 8:
                        pe.wait_ge(merged[m % 2], m // 2)
                    elif m >= 4:
                        pe.wait_ge(merged[m % 2], m // 2 - 1)
                    for i in range(8):
                        mm = pe.matmul(PS[:, merge_bank(m) + i // 4, (i % 4) * P:(i % 4 + 1) * P], w[:, 8 * (m % 8) + i, :], gates[:, :],
                                       start=True, stop=True)
                    mm.then_inc(merge_done, 1)

            def hidden_transpose(i):
                pe.wait_ge(htok_ready, i + 1)
                if i >= 2:
                    pe.wait_ge(biased, i - 1)
                elif i == 0:
                    pe.wait_ge(b1_ready, 1)
                for g in range(4):
                    c = (i % NQ) * 512 + g * P
                    mm = pe.transpose(PS[:, 6 + i % 2, g * P:(g + 1) * P], t1[:, c:c + P], ident)
                mm.then_inc(htrans_done, 1)

            def apply1(c, q):
                i = NQ * c + q
                if i >= 2:
                    pe.wait_ge(htok_ready, i - 1)
                for b in range(QI):
                    im = q * QI + b
                    mm = pe.matmul(PS[32 * (b % 4):32 * (b % 4) + 32, 4 + i % 2, (b // 4) * P:(b // 4 + 1) * P],
                                   t3[:, im * NS:im * NS + 32], wm[c % 2][:, im, :], start=True, stop=True)
                mm.then_inc(pre_done, 1)
                if i >= 1:
                    hidden_transpose(i - 1)

            def apply2(c, q):
                if q == 0:
                    pe.wait_ge(hid_ready, NQ * (c + 1))
                if c == 0:
                    if q < 2:
                        pe.wait_ge(htok_ready, NQ * NC - 1 + q)
                    else:
                        pe.wait_ge(biased, NQ * NC - 3 + q)
                if c == 0 and q == 0:
                    pe.wait_ge(pads_set, 6)
                    pe.wait_ge(gtok_done, 1)
                if c == 0:
                    for g in range(4):
                        im = q * QI + 4 * g
                        pe.matmul(PS[:, 4 + q, g * D:(g + 1) * D], gtok[:, im:im + 4, :].rearrange("p b q -> p (b q)"),
                                  C("tvb2", R), start=(g == 0), stop=False, skip_group_check=True)
                for b in range(QI):
                    im = q * QI + b
                    mm = pe.matmul(PS[32 * (b % 4):32 * (b % 4) + 32, 4 + q, (b // 4) * D:(b // 4 + 1) * D],
                                   hidv[:, c, im * NS:im * NS + 32], wm[c % 2][:, im, :],
                                   start=False, stop=(c == NC - 1), skip_group_check=True)
                if c == NC - 1:
                    mm.then_inc(ffn_done, 1)
                elif q == NQ - 1:
                    mm.then_inc(applied, 1)

            for cc in range(2 * NC + 1):
                if cc >= 1:
                    pe.wait_ge(merged[0], 4 * cc)
                    pe.wait_ge(merged[1], 4 * cc)
                for q in range(NQ):
                    if cc < 2 * NC:
                        merge(cc, q)
                    if (cc, q) == (1, 0):
                        for c in range(NC):
                            mm = pe.matmul(PS[:, 6, c * NI:(c + 1) * NI], C("tvb1", R)[:, c * P:(c + 1) * P], gate1, start=True, stop=True)
                        mm.then_inc(b1_done, 1)
                    if (cc, q) == (NC + 1, 0):
                        hidden_transpose(NQ * NC - 1)
                    if 1 <= cc <= NC:
                        apply1(cc - 1, q)
                    elif cc > NC:
                        apply2(cc - 1 - NC, q)


def _layout(np, i):
    f4 = np.float32
    a = {k: np.asarray(v) for k, v in i.items()}
    x = a["x"]
    xp = np.zeros((NI, x.shape[1] + 1, x.shape[2] + 1, 3), f4)
    xp[:, 1:, 1:] = x
    win = np.zeros((NI, 5, 5, 18, 18, 3), f4)
    for r in range(5):
        for c in range(5):
            win[:, r, c] = xp[:, 16 * r:16 * r + 18, 16 * c:16 * c + 18]
    k = 18 * 18 * 3
    xcol = np.zeros((KT * P, NTOK), f4)
    xcol[:k] = win.reshape(NTOK, k).T
    xcol[k] = 1.0
    xcol = xcol.reshape(KT, P, NTOK).transpose(1, 0, 2)
    parts = []
    for s in range(NSTEP):
        n = step_tokens(s)[0]
        parts.append(xcol[:, :, s * ST:s * ST + n].reshape(P, KT * n))
    w = a["L0_tok_conv_w"].reshape(16, 16, NSH, 3, D)
    w5 = np.zeros((18, 18, 3, NSH, D), f4)
    for g, (r, c) in enumerate(((1, 1), (1, 0), (1, 2), (0, 1), (2, 1))):
        w5[r:r + 16, c:c + 16, :, g] = w[:, :, g]
    wc = np.zeros((KT * P, NSH, D), f4)
    wc[:k] = w5.reshape(k, NSH, D)
    wc[k, 0] = a["L0_tok_conv_b"]
    wc = wc.reshape(KT, P, NSH * D).transpose(1, 0, 2).reshape(P, KT * NSH * D)

    cst = np.zeros((P, NCONST), f4)

    def put(name, v):
        lo, hi = COL[name]
        v = v.reshape(v.shape[0], -1)
        assert v.shape[1] == hi - lo, name
        cst[0:v.shape[0], lo:hi] = v
    put("dense_w", a["L0_tok_dense_w"])
    for name, src in (("q1", "Q1"), ("k1", "K1"), ("q2", "Q2"), ("k2", "K2"), ("v", "V"), ("o", "out")):
        put(name, a[f"L0_attn_{src}_w"].T)
    put("gfc1", a["L0_ffn_gfc1_w"].T)
    def rows(tv, base, first_only):
        v = np.zeros((R, base.size), f4)
        for t in range(len(TERMS)):
            for e in range(NE):
                for j in range(NJ):
                    if not first_only or (t, j) == (0, 0):
                        v[t * RE + e * NJ + j] = tv[e]
        for k in range(3 * NJ):
            if not first_only or k == 0:
                v[RB + k] = base
        return v
    put("gfc2", rows(a["L0_ffn_gfc2_w"], np.zeros(D, f4), False).T)
    gpart = np.zeros((R, 3), f4)
    for t, (_, gp) in enumerate(TERMS):
        gpart[t * RE:(t + 1) * RE, gp] = 1
    gpart[RB:, 0] = 1
    put("gpart", gpart)
    for name, src in (("gamma", "tok_gamma"), ("beta", "tok_beta"), ("dense_b", "tok_dense_b"), ("k1_b", "attn_K1_b"),
                      ("k2_b", "attn_K2_b"), ("gn_w", "attn_gn_w"), ("gn_b", "attn_gn_b"), ("out_b", "attn_out_b"),
                      ("gfc1_b", "ffn_gfc1_b")):
        put(name, a["L0_" + src].reshape(P, 1))
    put("gate_b", rows(a["L0_ffn_gfc2_b"], np.ones(1, f4), False))
    p = np.arange(P)
    put("even", (p // HD % 2 == 0).astype(f4).reshape(P, 1))
    put("odd", (p // HD % 2 == 1).astype(f4).reshape(P, 1))
    put("slice", np.tile(np.eye(NJ, dtype=f4), (R // NJ, 1)))
    put("tvb1", rows(a["L0_ffn_tv_b1"], a["L0_ffn_b1"], True))
    put("tvb2", rows(a["L0_ffn_tv_b2"], a["L0_ffn_b2"], True))
    put("ln_g", np.concatenate([a["L0_ffn_ln_g"][None], a["L0_ffn_tv_ln_g"]]))
    put("ln_b", np.concatenate([a["L0_ffn_ln_b"][None], a["L0_ffn_tv_ln_b"]]))
    coef = np.full((NE + 1, P), 0.03, f4)
    coef[0] = 1 - 0.03 * NE
    put("coef", coef)
    put("gnsum", (p[:, None] // 32 == p[None] // 32).astype(f4) / (32 * NS))
    put("ident", np.eye(P, dtype=f4))
    lam = np.concatenate([a["L0_attn_lambda_" + n].reshape(-1) for n in ("q1", "k1", "q2", "k2")])
    put("lam", np.broadcast_to(lam, (P, 4 * H)))

    def halves(tv, base):
        tv = tv.reshape(P, 2, HE)
        base = base.reshape(P, 2, HB)
        return [np.concatenate([tv[:, h], base[:, h]], 1) for h in range(2)]

    def w1(v):
        return v.reshape(-1, NC, NJ, SJ, D).transpose(0, 2, 1, 3, 4)

    def w2(v):
        return v.reshape(-1, NJ, SJ, NC, P).transpose(0, 1, 3, 2, 4)
    stages = halves(w1(a["L0_ffn_tv_W1"]), w1(a["L0_ffn_W1"])) + halves(w2(a["L0_ffn_tv_W2"]), w2(a["L0_ffn_W2"]))
    return {
        "consts": cst, "conv_filter": np.ascontiguousarray(wc), "windows": np.concatenate(parts, 1),
        "ffn_weights": np.stack(stages),
    }


def kernel(**inputs):
    import numpy as _np
    import concourse.bacc as _bacc
    from concourse import mybir as _mybir
    from concourse.bass_utils import run_bass_kernel_spmd as _run

    arrays = _layout(_np, inputs)
    nc = _bacc.Bacc("TRN2", target_bir_lowering=False, num_devices=1)
    f32 = _mybir.dt.float32
    d = {n: nc.dram_tensor(n, v.shape, f32, kind="ExternalInput").ap() for n, v in arrays.items()}
    out = nc.dram_tensor("out", (NTOK, D), f32, kind="ExternalOutput").ap()
    cols = [KT * ST * s for s in range(NSTEP)] + [KT * NTOK]
    xcol = [d["windows"][:, cols[s]:cols[s + 1]].rearrange("p (k n) -> p k n", k=KT) for s in range(NSTEP)]
    bf16 = _mybir.dt.bfloat16
    sce = nc.dram_tensor("parts_tv", (2, 3, P, 2 * HE), bf16, kind="Internal").ap()
    scb = nc.dram_tensor("parts_base", (2, 3, P, 2 * HB), bf16, kind="Internal").ap()
    build(nc, d["consts"], d["conv_filter"], xcol, d["ffn_weights"], sce, scb, out)
    r = _run(nc, [arrays], core_ids=[0])
    return r.results[0]["out"].reshape(NI, NS, D)
```
